# Optimizing a Trainium2 kernel written in Bass

```python
import numpy as np
import jax
import jax.numpy as jnp

def _softmax(x, axis=-1):
    return jax.nn.softmax(x, axis=axis)

def _gelu(x):
    return jax.nn.gelu(x, approximate=True)

def _silu(x):
    return jax.nn.silu(x)

def _sigmoid(x):
    return jax.nn.sigmoid(x)

def _layernorm(x, axis=-1, eps=1e-05):
    m = jnp.mean(x, axis=axis, keepdims=True)
    v = jnp.var(x, axis=axis, keepdims=True)
    return (x - m) / jnp.sqrt(v + eps)

def _scatter_add(tgt, idx, src, axis=0):
    return tgt.at[idx].add(src)

def _segment_sum(src, seg, n):
    return jax.ops.segment_sum(src, seg, n)
kernel_name = 'mk_cond_resid_d1_seqx_r4_bcbf13'

def setup_inputs(seed: int=0):
    np.random.seed(seed)
    _w = jnp.asarray

    def _rec_inputs():
        import jax
        import jax.numpy as jnp
        _rk = jax.random.key(seed)
        x = 7.22e-05 + 1 * jax.random.normal(jax.random.fold_in(_rk, 1), (16, 256, 256), jnp.float32)
        _lenS = 256 - jax.random.randint(jax.random.fold_in(_rk, 7), (16,), 0, max(1, 256 // 4) + 1, jnp.int32)
        _lenS2 = 256 - jax.random.randint(jax.random.fold_in(_rk, 8), (16,), 0, max(1, 256 // 4) + 1, jnp.int32)
        cond_512 = 0.0061147 + 1.02565 * jax.random.normal(jax.random.fold_in(_rk, 11), (16, 128), jnp.float32)
        return (x, cond_512)
    x, cond_512 = _rec_inputs()

    def _L0_cond_setup():
        import jax, jax.numpy as jnp
        import numpy as np
        import math
        HEAD_NUM = 16
        EPS = 1e-08

        def modulated_linear(x, s, aff_w, aff_b, w, b):
            style = s @ aff_w.T + aff_b
            w_mod = w[None, :, :] * style[:, None, :]
            demod = jax.lax.rsqrt(jnp.sum(w_mod * w_mod, axis=2) + EPS)
            w_mod = w_mod * demod[:, :, None]
            return jnp.einsum('bni,boi->bno', x, w_mod) + b
        key = jax.random.key(seed)
        ks = jax.random.split(key, 6)
        B, N, F, S = (8, 256, 256, 128)
        return {'x': jax.random.normal(ks[0], (B, N, F), dtype=jnp.float32), 's': jax.random.normal(ks[1], (B, S), dtype=jnp.float32), 'k_aff_w': jax.random.normal(ks[2], (F, S), dtype=jnp.float32) * 0.02, 'k_aff_b': jnp.ones((F,), dtype=jnp.float32), 'k_w': jax.random.normal(ks[3], (F, F), dtype=jnp.float32) * 0.02, 'k_b': jnp.zeros((F,), dtype=jnp.float32), 'o_aff_w': jax.random.normal(ks[4], (F, S), dtype=jnp.float32) * 0.02, 'o_aff_b': jnp.ones((F,), dtype=jnp.float32), 'o_w': jax.random.normal(ks[5], (F, F), dtype=jnp.float32) * 0.02, 'o_b': jnp.zeros((F,), dtype=jnp.float32)}
    _L0_cond_all = _L0_cond_setup()
    _L0_cond_in = {k: v for k, v in _L0_cond_all.items() if k in ('k_aff_w', 'k_aff_b', 'k_w', 'k_b', 'o_aff_w', 'o_aff_b', 'o_w', 'o_b')}
    del _L0_cond_all
    return {'x': x, 'cond_512': cond_512, 'L0_cond_k_aff_w': _L0_cond_in['k_aff_w'], 'L0_cond_k_aff_b': _L0_cond_in['k_aff_b'], 'L0_cond_k_w': _L0_cond_in['k_w'], 'L0_cond_k_b': _L0_cond_in['k_b'], 'L0_cond_o_aff_w': _L0_cond_in['o_aff_w'], 'L0_cond_o_aff_b': _L0_cond_in['o_aff_b'], 'L0_cond_o_w': _L0_cond_in['o_w'], 'L0_cond_o_b': _L0_cond_in['o_b']}

def reference(x, cond_512, L0_cond_k_aff_w, L0_cond_k_aff_b, L0_cond_k_w, L0_cond_k_b, L0_cond_o_aff_w, L0_cond_o_aff_b, L0_cond_o_w, L0_cond_o_b):
    import jax
    import jax.numpy as jnp

    def _L0_cond_ref(x, s, k_aff_w, k_aff_b, k_w, k_b, o_aff_w, o_aff_b, o_w, o_b):
        import jax, jax.numpy as jnp
        import numpy as np
        import math
        HEAD_NUM = 16
        EPS = 1e-08

        def modulated_linear(x, s, aff_w, aff_b, w, b):
            style = s @ aff_w.T + aff_b
            w_mod = w[None, :, :] * style[:, None, :]
            demod = jax.lax.rsqrt(jnp.sum(w_mod * w_mod, axis=2) + EPS)
            w_mod = w_mod * demod[:, :, None]
            return jnp.einsum('bni,boi->bno', x, w_mod) + b
        B, N, F = x.shape
        H = HEAD_NUM
        D = F // H
        kx = modulated_linear(x, s, k_aff_w, k_aff_b, k_w, k_b)
        kx = kx.reshape(B, N, H, D)
        q = k = v = kx
        scores = jnp.einsum('bnhd,bnjd->bnhj', q, k) / math.sqrt(D)
        A = jax.nn.softmax(scores, axis=-1)
        out = jnp.einsum('bnhj,bnjd->bnhd', A, v).reshape(B, N, F)
        out = modulated_linear(out, s, o_aff_w, o_aff_b, o_w, o_b)
        return out
    x = x + _L0_cond_ref(x, cond_512, L0_cond_k_aff_w, L0_cond_k_aff_b, L0_cond_k_w, L0_cond_k_b, L0_cond_o_aff_w, L0_cond_o_aff_b, L0_cond_o_w, L0_cond_o_b)
    return x

_drawn_inputs = setup_inputs


def setup_inputs(seed=0):
    import zlib

    import numpy as np

    out = dict(_drawn_inputs(seed))
    spreads = {'L0_cond_k_aff_b': (1.0, 0.2),
     'L0_cond_k_b': (0.0, 0.1),
     'L0_cond_o_aff_b': (1.0, 0.2),
     'L0_cond_o_b': (0.0, 0.1)}
    factors = {}
    for name, (base, spread) in spreads.items():
        noise = np.random.default_rng([zlib.crc32(name.encode()), seed]).standard_normal(out[name].shape)
        drawn = base * np.exp(spread * noise) if base else spread * noise
        out[name] = jnp.asarray(drawn.astype(out[name].dtype))
    for name, factor in factors.items():
        out[name] = (out[name] * factor).astype(out[name].dtype)
    return out
```

```python
from contextlib import ExitStack

import concourse.bass as bass
from concourse import mybir

BATCH, SEQ, FEAT, COND, HEADS = 16, 256, 256, 128, 16
DIM = FEAT // HEADS
P = 128
UNIT = 512
UNITS = BATCH * SEQ // UNIT
HALF_UNIT = UNIT // 2
BPU = UNIT // SEQ
CH = FEAT // P
PACK = P // DIM
OCTETS = UNIT // PACK
TILES = OCTETS // PACK
HT = TILES // 2
GROUPS = 4
STRIP = 32
PAD = DIM
DE = DIM + 1
EARLY = 3
PEEL = 2
EPS = 1e-8
SCALE = 1.0 / float(DIM) ** 0.5
ACT_TERMS = 4


def wait_positive(engine, semaphore, value):
    if not isinstance(value, int) or value > 0:
        engine.wait_ge(semaphore, value)


def build(nc, x, params, weights, y):
    fp32 = mybir.dt.float32
    ALU = mybir.AluOpType
    ACT = mybir.ActivationFunctionType
    AX = mybir.AxisListType

    k_scratch = nc.dram_tensor("k_scratch", (UNITS, PACK, FEAT, OCTETS), fp32, kind="Internal").ap()
    o_scratch = nc.dram_tensor("o_scratch", (UNITS, PACK, FEAT, OCTETS), fp32, kind="Internal").ap()

    ctx = ExitStack()
    with ctx:
        def sb(name, shape):
            return ctx.enter_context(nc.sbuf_tensor(name, shape, fp32))

        def pb(name, shape):
            return ctx.enter_context(nc.psum_tensor(name, shape, fp32))

        def sem(name):
            return ctx.enter_context(nc.semaphore(name))

        par = sb("par", [P, params.shape[1]])
        affine = par[:, 0:2 * FEAT].rearrange("c (m i) -> c m i", m=2)
        cond = par[:, 2 * FEAT:2 * FEAT + BATCH]
        at = 2 * FEAT + BATCH
        affine_bias = par[:, at:at + 4].rearrange("p (m c) -> p m c", m=2)
        out_bias = par[:, at + 4:at + 8].rearrange("p (m c) -> p m c", m=2)
        block_mask = par[:, at + 8:at + 8 + PACK]
        ident = par[:, at + 8 + PACK:at + 8 + PACK + P]
        wT = sb("wT", [P, 2, CH, FEAT])
        w_sq = sb("w_sq", [P, 2, CH, FEAT])
        style = sb("style", [P, 2, CH, BATCH])
        style_sq = sb("style_sq", [P, 2, CH, BATCH])
        var = sb("var", [P, 2, CH, BATCH])
        root = sb("root", [P, 2, CH, BATCH])
        inv0 = sb("inv0", [P, 2, CH, BATCH])
        newton = sb("newton", [P, 2, CH, BATCH])
        newton2 = sb("newton2", [P, 2, CH, BATCH])
        demod = sb("demod", [P, 2, CH, BATCH])

        xT = sb("xT", [P, UNITS, CH, UNIT])
        xs = sb("xs", [P, CH, UNIT])
        kT = sb("kT", [P, CH, UNIT])
        k_sd = sb("k_sd", [P, HEADS, OCTETS])
        k_sj = sb("k_sj", [P, DIM, OCTETS])
        k_stat = sb("k_stat", [P, PAD + OCTETS * STRIP])
        blocks1 = sb("blocks1", [P, PACK, OCTETS, HEADS])
        blocks2 = sb("blocks2", [P, PACK, OCTETS, DE])
        row_max = sb("row_max", [P, 2, HT, PACK])
        attn = sb("attn", [P, 2, HT, PACK, HEADS])
        a_stat = sb("a_stat", [P, PAD + OCTETS * STRIP])
        inv_sum = sb("inv_sum", [P, GROUPS, 2, PACK])
        mixed = sb("mixed", [P, DIM, PACK, TILES])
        oT = sb("oT", [P, CH, UNIT])
        os_ = sb("os", [P, CH, UNIT])
        yT = sb("yT", [P, CH, UNIT])

        proj = [pb(f"proj{c}", [P, UNIT]) for c in range(CH)]
        score = [pb(f"score{h}", [P, HT, PACK, HEADS]) for h in range(2)]
        turned = [pb(f"turned{h}", [P, HT, PACK, HEADS]) for h in range(2)]
        mix = [pb(f"mix{g}", [P, 2, PACK, DE]) for g in range(2)]

        k_cols = k_stat[:, PAD:].rearrange("p (n w) -> p n w", w=STRIP)[:, :, 0:HEADS]
        a_cols = a_stat[:, PAD:].rearrange("p (n w) -> p n w", w=STRIP)[:, :, 0:HEADS]

        params_loaded, weights_loaded = sem("params_loaded"), sem("weights_loaded")
        x_loaded = [sem(f"x_loaded{u}") for u in range(EARLY)]
        x_rest_loaded = sem("x_rest_loaded")
        style_summed, style_ready, style_squared = sem("style_summed"), sem("style_ready"), sem("style_squared")
        w_squared, var_summed, var_ready = sem("w_squared"), sem("var_summed"), sem("var_ready")
        root_ready, demod_step, demod_ready = sem("root_ready"), sem("demod_step"), sem("demod_ready")
        pads_zeroed, blocks_zeroed, ones_set = sem("pads_zeroed"), sem("blocks_zeroed"), sem("ones_set")
        xs_ready = sem("xs_ready")
        k_projected = [sem(f"k_projected{c}") for c in range(CH)]
        k_evacuated = [sem(f"k_evacuated{c}") for c in range(CH)]
        k_stored = [sem(f"k_stored{c}") for c in range(CH)]
        k_sd_loaded, k_sj_loaded = sem("k_sd_loaded"), sem("k_sj_loaded")
        k_stat_ready, blocks1_ready = sem("k_stat_ready"), sem("blocks1_ready")
        blocks2_act, blocks2_pool = sem("blocks2_act"), sem("blocks2_pool")
        scored, max_ready, centered, exp_ready = sem("scored"), sem("max_ready"), sem("centered"), sem("exp_ready")
        attn_turned, a_stat_ready = sem("attn_turned"), sem("a_stat_ready")
        mix_done, inv_ready, mix_divided = sem("mix_done"), sem("inv_ready"), sem("mix_divided")
        o_stored, oT_loaded, os_ready = sem("o_stored"), sem("oT_loaded"), sem("os_ready")
        y_projected = [sem(f"y_projected{c}") for c in range(CH)]
        y_evacuated = [sem(f"y_evacuated{c}") for c in range(CH)]
        y_added = [sem(f"y_added{c}") for c in range(CH)]
        y_stored = [sem(f"y_stored{c}") for c in range(CH)]

        block = ctx.enter_context(nc.Block())

        @block.sync
        def _(sp):
            sp.dma_start(par[:], params).then_inc(params_loaded, 16)
            for m in range(2):
                sp.dma_start(wT[:, m], weights[m].rearrange("(c p) o -> p c o", p=P)).then_inc(weights_loaded, 16)

            def counts(u):
                values = (u, u + 1, 2 * u, GROUPS * (u + 1), 16 * (u + 1))
                return values if isinstance(u, int) else tuple(sp.snap(sp.to_reg(v)) for v in values)

            def load_x(u):
                sp.dma_start(xT[:, u], x[u].rearrange("c p t -> p c t")).then_inc(x_loaded[u], 16)

            def turn_k(u):
                u, next_u, halves, _, dmas = counts(u)
                for c in range(CH):
                    sp.wait_ge(k_evacuated[c], next_u)
                    sp.dma_start(k_scratch[u, :, c * P:(c + 1) * P, :].rearrange("s p n -> p s n"),
                                 kT[:, c, :].rearrange("p (s n) -> p s n", s=PACK)).then_inc(k_stored[c], 16)
                for c in range(CH):
                    sp.wait_ge(k_stored[c], dmas)
                wait_positive(sp, blocks1_ready, halves)
                wait_positive(sp, k_stat_ready, halves)
                for s in range(PACK):
                    sp.dma_start(k_sd[DIM * s:DIM * (s + 1)],
                                 k_scratch[u, s].rearrange("(h d) n -> d h n", d=DIM)).then_inc(k_sd_loaded, 16)
                wait_positive(sp, blocks2_act, halves)
                wait_positive(sp, blocks2_pool, halves)
                sp.dma_start(k_sj[:].rearrange("p d n -> p (d n)"),
                             k_scratch[u].rearrange("s (j d) n -> (s j) (d n)", d=DIM)).then_inc(k_sj_loaded, 16)

            def turn_o(u):
                u, _, _, groups, dmas = counts(u)
                sp.wait_ge(mix_divided, groups)
                sp.dma_start(o_scratch[u].rearrange("v (h d) n -> (v h) (d n)", d=DIM),
                             mixed[:].rearrange("p d s t -> p (d s t)")).then_inc(o_stored, 16)
                sp.wait_ge(o_stored, dmas)
                wait_positive(sp, os_ready, u)
                for c in range(CH):
                    sp.dma_start(oT[:, c, :].rearrange("p (v n) -> p v n", v=PACK),
                                 o_scratch[u, :, c * P:(c + 1) * P, :].rearrange("v p n -> p v n")
                                 ).then_inc(oT_loaded, 16)

            def store_y(u):
                u, next_u, _, _, _ = counts(u)
                for c in range(CH):
                    sp.wait_ge(y_added[c], next_u)
                    sp.dma_start(y[u, c], yT[:, c, :]).then_inc(y_stored[c], 16)

            for u in range(EARLY):
                load_x(u)
            turn_k(0)
            sp.dma_start(xT[:, EARLY:UNITS].rearrange("p u c t -> p (u c) t"),
                         x[EARLY:UNITS].rearrange("u c p t -> p (u c) t")).then_inc(x_rest_loaded, 16)
            turn_k(1)

            def unit(u, ahead, behind):
                if ahead:
                    turn_k(u + 2)
                if behind:
                    store_y(u - 1)
                turn_o(u)

            for u in range(PEEL):
                unit(u, True, u > 0)
            with sp.Fori(PEEL, UNITS - 2) as u:
                unit(u, True, True)
            for u in range(UNITS - 2, UNITS):
                unit(u, False, True)
            store_y(UNITS - 1)
            for c in range(CH):
                sp.wait_ge(y_stored[c], 16 * UNITS)

        @block.tensor
        def _(pe):
            pe.wait_ge(params_loaded, 16)
            for m in range(2):
                for c in range(CH):
                    q = (m * CH + c) * BATCH
                    last = pe.matmul(proj[0][:, q:q + BATCH], affine[:, m, c * P:(c + 1) * P], cond,
                                     start=True, stop=True)
            last.then_inc(style_summed, 1)
            pe.wait_ge(style_squared, 1)
            pe.wait_ge(w_squared, 1)
            for m in range(2):
                for c in range(CH):
                    q = (m * CH + c) * BATCH
                    for i in range(CH):
                        last = pe.matmul(proj[1][:, q:q + BATCH], w_sq[:, m, i, c * P:(c + 1) * P],
                                         style_sq[:, m, i, :], start=(i == 0), stop=(i == CH - 1))
            last.then_inc(var_summed, 1)

            def project(u, c):
                pe.wait_ge(xs_ready, u + 1)
                for i in range(CH):
                    last = pe.matmul(proj[c][:], wT[:, 0, i, c * P:(c + 1) * P], xs[:, i, :],
                                     start=(i == 0), stop=(i == CH - 1))
                last.then_inc(k_projected[c], 1)

            def finish(u, c):
                pe.wait_ge(os_ready, u + 1)
                for i in range(CH):
                    last = pe.matmul(proj[c][:], wT[:, 1, i, c * P:(c + 1) * P], os_[:, i, :],
                                     start=(i == 0), stop=(i == CH - 1))
                last.then_inc(y_projected[c], 1)

            def scores(u, h):
                pe.wait_ge(k_stat_ready, 2 * u + h + 1)
                pe.wait_ge(blocks1_ready, 2 * u + h + 1)
                wait_positive(pe, centered, 2 * u + h - 1)
                for t in range(HT):
                    for half in range(2):
                        for strip in range(4):
                            n = (h * HT + t) * PACK + 2 * strip + half
                            col = PAD + n * STRIP - half * PAD
                            last = pe.matmul(score[h][STRIP * strip:STRIP * (strip + 1), t], k_stat[:, col:col + STRIP],
                                             blocks1[:, :, n, :], start=(half == 0), stop=(half == 1))
                last.then_inc(scored, 1)

            def turn(u, h):
                pe.wait_ge(exp_ready, 2 * u + h + 1)
                wait_positive(pe, a_stat_ready, 2 * u + h - 1)
                for t in range(HT):
                    last = pe.transpose(turned[h][:, t].rearrange("p s h -> p (s h)"),
                                        attn[:, h, t].rearrange("p s j -> p (s j)"), ident)
                last.then_inc(attn_turned, 1)

            def mix_values(u, h):
                pe.wait_ge(a_stat_ready, 2 * u + h + 1)
                pe.wait_ge(blocks2_act, 2 * u + h + 1)
                pe.wait_ge(blocks2_pool, 2 * u + h + 1)
                for k in range(2):
                    g = 2 * h + k
                    wait_positive(pe, mix_divided, GROUPS * u + g - 1)
                    for t in range(2):
                        for half in range(2):
                            for strip in range(4):
                                n = (2 * g + t) * PACK + 2 * strip + half
                                col = PAD + n * STRIP - half * PAD
                                last = pe.matmul(mix[g % 2][STRIP * strip:STRIP * (strip + 1), t], a_stat[:, col:col + STRIP],
                                                 blocks2[:, :, n, :], start=(half == 0), stop=(half == 1))
                    last.then_inc(mix_done, 1)

            pe.wait_ge(style_ready, 4)
            pe.wait_ge(var_ready, 1)
            for u in range(2):
                for c in range(CH):
                    if u > 0:
                        pe.wait_ge(k_evacuated[c], u)
                    project(u, c)

            def unit(u, ahead, behind):
                scores(u, 0)
                scores(u, 1)
                if ahead:
                    pe.wait_ge(k_evacuated[0], u + 2)
                    if behind:
                        wait_positive(pe, y_evacuated[0], u - 1)
                    project(u + 2, 0)
                turn(u, 0)
                if ahead:
                    pe.wait_ge(k_evacuated[1], u + 2)
                    if behind:
                        wait_positive(pe, y_evacuated[1], u - 1)
                    project(u + 2, 1)
                turn(u, 1)
                mix_values(u, 0)
                mix_values(u, 1)
                if behind:
                    for c in range(CH):
                        pe.wait_ge(k_evacuated[c], u + 3 if ahead else UNITS)
                        wait_positive(pe, y_evacuated[c], u - 1)
                        finish(u - 1, c)

            for u in range(PEEL):
                unit(u, True, u > 0)
            with pe.Fori(PEEL, UNITS - 2) as u:
                unit(u, True, True)
            for u in range(UNITS - 2, UNITS):
                unit(u, False, True)
            for c in range(CH):
                pe.wait_ge(y_evacuated[c], UNITS - 1)
                finish(UNITS - 1, c)

        @block.vector
        def _(dve):
            dve.memset(k_stat[:], 0.0).then_inc(pads_zeroed, 1)
            dve.memset(blocks1[:], 0.0).then_inc(blocks_zeroed, 1)
            dve.wait_ge(style_summed, 1)
            for m in range(2):
                for c in range(CH):
                    q = (m * CH + c) * BATCH
                    dve.tensor_scalar(style[:, m, c, :], proj[0][:, q:q + BATCH], affine_bias[:, m, c:c + 1], None,
                                      ALU.add).then_inc(style_ready, 1)
            dve.wait_ge(style_ready, 4)
            dve.tensor_tensor(style_sq[:], style[:], style[:], ALU.mult).then_inc(style_squared, 1)

            def scale_x(u):
                for c in range(CH):
                    wait_positive(dve, k_projected[c], u)
                early = isinstance(u, int) and u < EARLY
                dve.wait_ge(x_loaded[u] if early else x_rest_loaded, 16)
                for i in range(CH):
                    for b in range(BPU):
                        last = dve.tensor_scalar(xs[:, i, b * SEQ:(b + 1) * SEQ], xT[:, u, i, b * SEQ:(b + 1) * SEQ],
                                                 style[:, 0, i, bass.ds(BPU * u + b, 1)], None, ALU.mult)
                last.then_inc(xs_ready, 1)

            scale_x(0)
            dve.wait_ge(var_summed, 1)
            dve.tensor_scalar(var[:].rearrange("p m c b -> p (m c b)"), proj[1][:, 0:2 * CH * BATCH], EPS, None,
                              ALU.add).then_inc(var_ready, 1)
            dve.wait_ge(root_ready, 1)
            dve.reciprocal(inv0[:], root[:]).then_inc(demod_step, 1)
            dve.wait_ge(demod_step, 1)
            dve.tensor_tensor(newton[:], inv0[:], inv0[:], ALU.mult).then_inc(demod_step, 1)
            dve.wait_ge(demod_step, 2)
            dve.tensor_tensor(newton2[:], newton[:], var[:], ALU.mult).then_inc(demod_step, 1)
            dve.wait_ge(demod_step, 3)
            dve.tensor_scalar(newton[:], newton2[:], -0.5, 1.5, ALU.mult, ALU.add).then_inc(demod_step, 1)
            dve.wait_ge(demod_step, 4)
            dve.tensor_tensor(demod[:], newton[:], inv0[:], ALU.mult).then_inc(demod_ready, 1)

            def spread_stat(u, h):
                dve.wait_ge(k_sd_loaded, PACK * 16 * (u + 1))
                wait_positive(dve, scored, 2 * u + h - 1)
                n0 = h * OCTETS // 2
                dve.tensor_copy(k_cols[:, n0:n0 + OCTETS // 2, :],
                                 k_sd[:, :, n0:n0 + OCTETS // 2].rearrange("p h n -> p n h")).then_inc(k_stat_ready, 1)

            def spread1(u, h):
                dve.wait_ge(k_sd_loaded, PACK * 16 * (u + 1))
                wait_positive(dve, scored, 2 * u + h - 1)
                n0 = h * OCTETS // 2
                for s in range(PACK):
                    last = dve.tensor_scalar(blocks1[:, s, n0:n0 + OCTETS // 2, :],
                                             k_sd[:, :, n0:n0 + OCTETS // 2].rearrange("p h n -> p n h"),
                                             block_mask[:, s:s + 1], None, ALU.mult)
                last.then_inc(blocks1_ready, 1)

            def center(u, h):
                dve.wait_ge(scored, 2 * u + h + 1)
                dve.tensor_reduce(row_max[:, h], score[h][:], AX.X, ALU.max).then_inc(max_ready, 1)
                dve.wait_ge(max_ready, 2 * u + h + 1)
                wait_positive(dve, attn_turned, 2 * u + h - 1)
                dve.tensor_tensor(attn[:, h].rearrange("p t s j -> p (t s) j"), score[h][:].rearrange("p t s j -> p (t s) j"),
                                  row_max[:, h].rearrange("p t s -> p (t s)").unsqueeze(2).to_broadcast([P, HT * PACK, HEADS]),
                                  ALU.subtract).then_inc(centered, 1)

            def divide(u, g):
                dve.wait_ge(mix_done, GROUPS * u + g + 1)
                dve.reciprocal(inv_sum[:, g], mix[g % 2][:, :, :, DIM]).then_inc(inv_ready, 1)
                dve.wait_ge(inv_ready, GROUPS * u + g + 1)
                if g == 0:
                    wait_positive(dve, o_stored, 16 * u)
                dve.tensor_tensor(mixed[:, :, :, 2 * g:2 * g + 2].rearrange("p d s t -> p t s d"),
                                  mix[g % 2][:, :, :, 0:DIM],
                                  inv_sum[:, g].unsqueeze(3).to_broadcast([P, 2, PACK, DIM]),
                                  ALU.mult).then_inc(mix_divided, 1)

            def scale_o(u):
                dve.wait_ge(oT_loaded, CH * 16 * (u + 1))
                for c in range(CH):
                    wait_positive(dve, y_projected[c], u)
                for i in range(CH):
                    for b in range(BPU):
                        dst = os_[:, i, :].rearrange("p (v r) -> p v r", v=PACK)[:, :, b * OCTETS // 2:(b + 1) * OCTETS // 2]
                        src = oT[:, i, :].rearrange("p (v r) -> p v r", v=PACK)[:, :, b * OCTETS // 2:(b + 1) * OCTETS // 2]
                        last = dve.tensor_scalar(dst, src, style[:, 1, i, bass.ds(BPU * u + b, 1)], None, ALU.mult)
                last.then_inc(os_ready, 1)

            dve.wait_ge(blocks_zeroed, 1)
            scale_x(1)
            for h in range(2):
                spread_stat(0, h)
                spread1(0, h)
            scale_x(2)

            def unit(u, ahead, behind):
                center(u, 0)
                center(u, 1)
                if ahead or behind == "last but one":
                    spread_stat(u + 1, 0)
                    spread1(u + 1, 0)
                if ahead == "more":
                    scale_x(u + 3)
                divide(u, 0)
                divide(u, 1)
                if behind:
                    scale_o(u - 1)
                if ahead or behind == "last but one":
                    spread_stat(u + 1, 1)
                    spread1(u + 1, 1)
                divide(u, 2)
                divide(u, 3)

            for u in range(PEEL):
                unit(u, "more", "yes" if u > 0 else None)
            with dve.Fori(PEEL, UNITS - 3) as u:
                unit(u, "more", "yes")
            unit(UNITS - 3, "spread", "yes")
            unit(UNITS - 2, None, "last but one")
            unit(UNITS - 1, None, "yes")
            scale_o(UNITS - 1)

        @block.gpsimd
        def _(pool):
            pool.memset(a_stat[:], 0.0).then_inc(pads_zeroed, 1)
            pool.memset(blocks2[:], 0.0).then_inc(blocks_zeroed, 1)
            pool.wait_ge(params_loaded, 16)
            pool.wait_ge(blocks_zeroed, 2)
            pool.wait_ge(pads_zeroed, 2)
            for s in range(PACK):
                pool.tensor_copy(blocks2[:, s, :, DIM], block_mask[:, s:s + 1].to_broadcast([P, OCTETS])
                                 ).then_inc(ones_set, 1)

            def spread2(u, h):
                pool.wait_ge(k_sj_loaded, 16 * (u + 1))
                wait_positive(pool, mix_done, GROUPS * u + 2 * h - 2)
                n0 = h * OCTETS // 2
                for s in range(ACT_TERMS, PACK):
                    last = pool.tensor_tensor(blocks2[:, s, n0:n0 + OCTETS // 2, 0:DIM],
                                              k_sj[:, :, n0:n0 + OCTETS // 2].rearrange("p d n -> p n d"),
                                              block_mask[:, s:s + 1].unsqueeze(2).to_broadcast([P, OCTETS // 2, DIM]),
                                              ALU.mult)
                last.then_inc(blocks2_pool, 1)

            def add_x(u):
                for c in range(CH):
                    pool.wait_ge(y_evacuated[c], u + 1)
                    y_view = yT[:, c, :].rearrange("p (v r) -> p v r", v=PACK)
                    pool.tensor_tensor(y_view, y_view, xT[:, u, c, :].rearrange("p (r v) -> p v r", v=PACK),
                                       ALU.add).then_inc(y_added[c], 1)

            for h in range(2):
                spread2(0, h)

            def unit(u, ahead, behind):
                if ahead:
                    spread2(u + 1, 0)
                    spread2(u + 1, 1)
                if behind:
                    add_x(u - 1)

            for u in range(PEEL):
                unit(u, True, u > 0)
            with pool.Fori(PEEL, UNITS - 1) as u:
                unit(u, True, True)
            unit(UNITS - 1, False, True)
            add_x(UNITS - 1)

        @block.scalar
        def _(act):
            act.wait_ge(weights_loaded, 32)
            act.activation(w_sq[:], wT[:], ACT.Square).then_inc(w_squared, 1)
            act.wait_ge(var_ready, 1)
            act.activation(root[:], var[:], ACT.Sqrt).then_inc(root_ready, 1)
            act.wait_ge(demod_ready, 1)

            def evacuate_k(u, c):
                act.wait_ge(k_projected[c], u + 1)
                wait_positive(act, k_stored[c], 16 * u)
                for b in range(BPU):
                    q = BPU * u + b
                    last = act.activation(kT[:, c, b * SEQ:(b + 1) * SEQ], proj[c][:, b * SEQ:(b + 1) * SEQ], ACT.Identity,
                                          bias=out_bias[:, 0, c:c + 1], scale=demod[:, 0, c, bass.ds(q, 1)])
                last.then_inc(k_evacuated[c], 1)

            def exponent(u, h):
                act.wait_ge(centered, 2 * u + h + 1)
                act.activation(attn[:, h], attn[:, h], ACT.Exp, scale=SCALE).then_inc(exp_ready, 1)

            def copy_turned(u, h):
                act.wait_ge(attn_turned, 2 * u + h + 1)
                wait_positive(act, mix_done, GROUPS * u + 2 * h - 2)
                n0 = h * OCTETS // 2
                act.activation(a_cols[:, n0:n0 + OCTETS // 2, :], turned[h][:].rearrange("p t v h -> p (t v) h"),
                               ACT.Copy).then_inc(a_stat_ready, 1)

            def spread2(u, h):
                act.wait_ge(k_sj_loaded, 16 * (u + 1))
                wait_positive(act, mix_done, GROUPS * u + 2 * h - 2)
                n0 = h * OCTETS // 2
                for s in range(ACT_TERMS):
                    last = act.activation(blocks2[:, s, n0:n0 + OCTETS // 2, 0:DIM],
                                          k_sj[:, :, n0:n0 + OCTETS // 2].rearrange("p d n -> p n d"),
                                          ACT.Copy, scale=block_mask[:, s:s + 1])
                last.then_inc(blocks2_act, 1)

            def evacuate_y(u, c):
                act.wait_ge(y_projected[c], u + 1)
                wait_positive(act, y_stored[c], 16 * u)
                for b in range(BPU):
                    q = BPU * u + b
                    half = slice(b * OCTETS // 2, (b + 1) * OCTETS // 2)
                    last = act.activation(yT[:, c, :].rearrange("p (v r) -> p v r", v=PACK)[:, :, half],
                                          proj[c][:].rearrange("p (v r) -> p v r", v=PACK)[:, :, half], ACT.Identity,
                                          bias=out_bias[:, 1, c:c + 1], scale=demod[:, 1, c, bass.ds(q, 1)])
                last.then_inc(y_evacuated[c], 1)

            for u in range(2):
                for c in range(CH):
                    evacuate_k(u, c)
            act.wait_ge(pads_zeroed, 2)
            act.wait_ge(ones_set, PACK)
            for h in range(2):
                spread2(0, h)

            def unit(u, ahead, behind):
                exponent(u, 0)
                if ahead:
                    evacuate_k(u + 2, 0)
                exponent(u, 1)
                copy_turned(u, 0)
                if ahead:
                    evacuate_k(u + 2, 1)
                copy_turned(u, 1)
                if ahead or behind == "last but one":
                    spread2(u + 1, 0)
                    spread2(u + 1, 1)
                if behind:
                    for c in range(CH):
                        evacuate_y(u - 1, c)

            for u in range(PEEL):
                unit(u, True, "yes" if u > 0 else None)
            with act.Fori(PEEL, UNITS - 2) as u:
                unit(u, True, "yes")
            unit(UNITS - 2, False, "last but one")
            unit(UNITS - 1, False, "yes")
            for c in range(CH):
                evacuate_y(UNITS - 1, c)


def kernel(x, cond_512, L0_cond_k_aff_w, L0_cond_k_aff_b, L0_cond_k_w, L0_cond_k_b,
           L0_cond_o_aff_w, L0_cond_o_aff_b, L0_cond_o_w, L0_cond_o_b):
    import numpy as np
    import concourse.bacc as bacc
    from concourse.bass_utils import run_bass_kernel_spmd

    fp32 = mybir.dt.float32
    x_in = np.ascontiguousarray(np.asarray(x).reshape(UNITS, UNIT, CH, P).transpose(0, 2, 3, 1))

    def column(v):
        return np.asarray(v).reshape(CH, P).T

    mask = np.repeat(np.eye(PACK, dtype=np.float32), DIM, axis=0)
    params = np.ascontiguousarray(np.concatenate([
        np.asarray(L0_cond_k_aff_w).T, np.asarray(L0_cond_o_aff_w).T, np.asarray(cond_512).T,
        column(L0_cond_k_aff_b), column(L0_cond_o_aff_b), column(L0_cond_k_b), column(L0_cond_o_b),
        mask, np.eye(P, dtype=np.float32)], axis=1))
    weights = np.ascontiguousarray(np.stack([np.asarray(L0_cond_k_w).T, np.asarray(L0_cond_o_w).T]))

    nc = bacc.Bacc("TRN2", target_bir_lowering=False, num_devices=1)
    arrays = {"x_in": x_in, "params": params, "weights": weights}
    aps = [nc.dram_tensor(name, a.shape, fp32, kind="ExternalInput").ap() for name, a in arrays.items()]
    y = nc.dram_tensor("y", (UNITS, CH, P, UNIT), fp32, kind="ExternalOutput").ap()
    build(nc, *aps, y)
    result = run_bass_kernel_spmd(nc, [arrays], core_ids=[0])
    out = result.results[0]["y"].reshape(UNITS, FEAT, PACK, PACK, TILES)
    return np.ascontiguousarray(out.transpose(0, 3, 4, 2, 1)).reshape(BATCH, SEQ, FEAT)
```

```python
from contextlib import ExitStack

import concourse.bass as bass
from concourse import mybir

BATCH, SEQ, FEAT, COND, HEADS = 16, 256, 256, 128, 16
DIM = FEAT // HEADS
P = 128
UNIT = 512
UNITS = BATCH * SEQ // UNIT
HALF_UNIT = UNIT // 2
BPU = UNIT // SEQ
CH = FEAT // P
PACK = P // DIM
OCTETS = UNIT // PACK
TILES = OCTETS // PACK
HT = TILES // 2
GROUPS = 4
STRIP = 32
PAD = DIM
DE = DIM + 1
EARLY_X = 7
AHEAD = 5
PHASE = UNITS - AHEAD
LAST = UNITS - 1
EPS = 1e-8
SCALE = 1.0 / float(DIM) ** 0.5
DVE_TERMS = 5
ACT_TERMS_FIRST = 2
ACT_TERMS = 4


def wait_positive(engine, semaphore, value):
    if not isinstance(value, int) or value > 0:
        engine.wait_ge(semaphore, value)


def build(nc, x, params, weights, y, y_last):
    fp32 = mybir.dt.float32
    ALU = mybir.AluOpType
    ACT = mybir.ActivationFunctionType
    AX = mybir.AxisListType

    k_scratch = nc.dram_tensor("k_scratch", (UNITS, PACK, FEAT, OCTETS), fp32, kind="Internal").ap()
    o_scratch = nc.dram_tensor("o_scratch", (UNITS, PACK, FEAT, OCTETS), fp32, kind="Internal").ap()
    o_last = nc.dram_tensor("o_last", (2, PACK, FEAT, OCTETS // 2), fp32, kind="Internal").ap()

    ctx = ExitStack()
    with ctx:
        def sb(name, shape):
            return ctx.enter_context(nc.sbuf_tensor(name, shape, fp32))

        def pb(name, shape):
            return ctx.enter_context(nc.psum_tensor(name, shape, fp32))

        def sem(name):
            return ctx.enter_context(nc.semaphore(name))

        head = FEAT + BATCH + 2 * 2 * CH + PACK
        par = sb("par", [P, params.shape[1]])
        affine = [par[:, 0:FEAT], par[:, head:head + FEAT]]
        cond = par[:, FEAT:FEAT + BATCH]
        at = FEAT + BATCH
        affine_bias = par[:, at:at + 4].rearrange("p (m c) -> p m c", m=2)
        out_bias = par[:, at + 4:at + 8].rearrange("p (m c) -> p m c", m=2)
        block_mask = par[:, at + 8:head]
        ident = par[:, head + FEAT:head + FEAT + P]
        wT = sb("wT", [P, 2, CH, FEAT])
        w_sq = sb("w_sq", [P, 2, CH, FEAT])
        style = sb("style", [P, 2, CH, BATCH])
        style_sq = sb("style_sq", [P, 2, CH, BATCH])
        var = sb("var", [P, 2, CH, BATCH])
        root = sb("root", [P, 2, CH, BATCH])
        inv0 = sb("inv0", [P, 2, CH, BATCH])
        newton = sb("newton", [P, 2, CH, BATCH])
        newton2 = sb("newton2", [P, 2, CH, BATCH])
        demod = sb("demod", [P, 2, CH, BATCH])

        xT = sb("xT", [P, UNITS, CH, UNIT])
        xs = sb("xs", [P, 2, CH, UNIT])
        kT = sb("kT", [P, AHEAD, CH, UNIT])
        k_sd = sb("k_sd", [P, HEADS, OCTETS])
        k_sj = sb("k_sj", [P, DIM, OCTETS])
        k_stat = sb("k_stat", [P, PAD + OCTETS * STRIP])
        blocks1 = sb("blocks1", [P, PACK, OCTETS, HEADS])
        blocks2 = sb("blocks2", [P, PACK, OCTETS, DE])
        row_max = sb("row_max", [P, 2, HT, PACK])
        attn = sb("attn", [P, 2, HT, PACK, HEADS])
        k_sjc = sb("k_sjc", [P, OCTETS, DIM])
        a_stat = sb("a_stat", [P, PAD + OCTETS * STRIP])
        inv_sum = sb("inv_sum", [P, GROUPS, 2, PACK])
        mixed = sb("mixed", [P, DIM, PACK, TILES])
        oT = sb("oT", [P, CH, UNIT])
        os_ = sb("os", [P, CH, UNIT])
        yT = sb("yT", [P, CH, UNIT])
        x_last = sb("x_last", [P, CH, UNIT])

        proj = [pb(f"proj{c}", [P, UNIT]) for c in range(CH)]
        score = [pb(f"score{h}", [P, HT, PACK, HEADS]) for h in range(2)]
        turned = [pb(f"turned{h}", [P, HT, PACK, HEADS]) for h in range(2)]
        mix = [pb(f"mix{g}", [P, 2, PACK, DE]) for g in range(2)]

        mixed_halves = mixed[:].rearrange("p d s t -> p (d s t)").rearrange("p (a d s t) -> p a d s t", a=2, d=DIM, s=PACK)
        y_banks = [[proj[c][:, 0:HALF_UNIT] for c in range(CH)],
                   [score[c][:].rearrange("p t s j -> p (t s j)")[:, 0:HALF_UNIT] for c in range(CH)]]

        def half_view(buffer, h, c):
            return buffer[:, c, h * HALF_UNIT:(h + 1) * HALF_UNIT].rearrange("p (v n) -> p v n", v=PACK)

        style_sum = turned[0][:, 0].rearrange("p s h -> p (s h)")[:, 0:2 * CH * BATCH].rearrange(
            "p (m c b) -> p m c b", m=2, c=CH)
        var_sum = turned[1][:, 0].rearrange("p s h -> p (s h)")[:, 0:2 * CH * BATCH].rearrange(
            "p (m c b) -> p m c b", m=2, c=CH)

        k_cols = k_stat[:, PAD:].rearrange("p (n w) -> p n w", w=STRIP)[:, :, 0:HEADS]
        a_cols = a_stat[:, PAD:].rearrange("p (n w) -> p n w", w=STRIP)[:, :, 0:HEADS]

        params_loaded, ident_loaded = sem("params_loaded"), sem("ident_loaded")
        weights_loaded = [sem(f"weights_loaded{m}") for m in range(2)]
        x_loaded = [sem(f"x_loaded{u}") for u in range(UNITS)]
        style_summed, style_ready, style_squared = sem("style_summed"), sem("style_ready"), sem("style_squared")
        w_squared, var_summed, var_ready = sem("w_squared"), sem("var_summed"), sem("var_ready")
        root_ready, demod_step, demod_ready = sem("root_ready"), sem("demod_step"), sem("demod_ready")
        pads_zeroed, blocks_zeroed, ones_set = sem("pads_zeroed"), sem("blocks_zeroed"), sem("ones_set")
        xs_ready = sem("xs_ready")
        k_projected = [sem(f"k_projected{c}") for c in range(CH)]
        k_evacuated = [sem(f"k_evacuated{c}") for c in range(CH)]
        k_stored = [sem(f"k_stored{c}") for c in range(CH)]
        k_sd_loaded, k_sj_loaded = sem("k_sd_loaded"), sem("k_sj_loaded")
        k_stat_ready, blocks1_ready = sem("k_stat_ready"), sem("blocks1_ready")
        blocks1_act = sem("blocks1_act")
        k_sj_copied = sem("k_sj_copied")
        blocks2_act, blocks2_pool = sem("blocks2_act"), sem("blocks2_pool")
        scored, max_ready, centered, exp_ready = sem("scored"), sem("max_ready"), sem("centered"), sem("exp_ready")
        attn_turned, a_stat_ready = sem("attn_turned"), sem("a_stat_ready")
        mix_done, inv_ready, mix_divided = sem("mix_done"), sem("inv_ready"), sem("mix_divided")
        o_stored, oT_loaded, os_ready = sem("o_stored"), sem("oT_loaded"), sem("os_ready")
        y_projected = [sem(f"y_projected{c}") for c in range(CH)]
        y_evacuated = [sem(f"y_evacuated{c}") for c in range(CH)]
        y_added = [sem(f"y_added{c}") for c in range(CH)]
        y_stored = [sem(f"y_stored{c}") for c in range(CH)]

        halves_stored = [sem(f"half{h}_stored") for h in range(2)]
        halves_loaded = [sem(f"half{h}_loaded") for h in range(2)]
        x_biased, halves_scaled, halves_finished = sem("x_biased"), sem("halves_scaled"), sem("halves_finished")
        halves_added, y_last_stored = sem("halves_added"), sem("y_last_stored")

        block = ctx.enter_context(nc.Block())

        @block.sync
        def _(sp):
            sp.dma_start(par[:, 0:head], params[:, 0:head]).then_inc(params_loaded, 16)

            def load_w(m):
                sp.dma_start(wT[:, m], weights[m].rearrange("(c p) o -> p c o", p=P)).then_inc(weights_loaded[m], 16)

            def counts(u):
                values = (u, u + 1, 2 * u, GROUPS * (u + 1), 16 * (u + 1))
                return values if isinstance(u, int) else tuple(sp.snap(sp.to_reg(v)) for v in values)

            def load_x(u):
                sp.dma_start(xT[:, u], x[u].rearrange("c p t -> p c t")).then_inc(x_loaded[u], 16)

            def load_sd(u):
                u, _, halves, _, dmas = counts(u)
                for c in range(CH):
                    sp.wait_ge(k_stored[c], dmas)
                wait_positive(sp, k_stat_ready, halves)
                for s in range(PACK):
                    sp.dma_start(k_sd[DIM * s:DIM * (s + 1)],
                                 k_scratch[u, s].rearrange("(h d) n -> d h n", d=DIM)).then_inc(k_sd_loaded, 16)

            def load_sj(u):
                u, _, halves, _, dmas = counts(u)
                for c in range(CH):
                    sp.wait_ge(k_stored[c], dmas)
                wait_positive(sp, k_sj_copied, u)
                sp.dma_start(k_sj[:].rearrange("p d n -> p (d n)"),
                             k_scratch[u].rearrange("s (j d) n -> (s j) (d n)", d=DIM)).then_inc(k_sj_loaded, 16)

            def store_o(u):
                u, _, _, groups, _ = counts(u)
                sp.wait_ge(mix_divided, groups)
                sp.dma_start(o_scratch[u].rearrange("v (h d) n -> (v h) (d n)", d=DIM),
                             mixed[:].rearrange("p d s t -> p (d s t)")).then_inc(o_stored, 16)

            def load_o(u):
                u, _, _, _, dmas = counts(u)
                sp.wait_ge(o_stored, dmas)
                wait_positive(sp, os_ready, u)
                for c in range(CH):
                    sp.dma_start(oT[:, c, :].rearrange("p (v n) -> p v n", v=PACK),
                                 o_scratch[u, :, c * P:(c + 1) * P, :].rearrange("v p n -> p v n")
                                 ).then_inc(oT_loaded, 16)

            def store_y(u):
                u, next_u, _, _, _ = counts(u)
                for c in range(CH):
                    sp.wait_ge(y_added[c], next_u)
                    sp.dma_start(y[u, c], yT[:, c, :]).then_inc(y_stored[c], 16)

            load_w(0)
            load_x(0)
            sp.dma_start(par[:, head:], params[:, head:]).then_inc(ident_loaded, 16)
            load_x(1)
            load_w(1)
            load_x(2)
            load_x(3)
            load_x(4)
            load_x(5)
            load_sd(0)
            load_sj(0)
            load_sd(1)
            load_sj(1)
            load_x(6)
            load_sd(2)

            def unit(u, sd=True):
                store_o(u - 1)
                load_sj(u + 1)
                load_o(u - 1)
                if sd:
                    load_sd(u + 2)
                if not isinstance(u, int) or u > 1:
                    store_y(u - 2)

            for u in range(1, UNITS - EARLY_X + 1):
                unit(u)
                load_x(u + EARLY_X - 1)
            with sp.Fori(UNITS - EARLY_X + 1, LAST - 1) as u:
                unit(u)
            unit(LAST - 1, sd=False)

            def store_half(h):
                sp.wait_ge(mix_divided, GROUPS * LAST + 2 * (h + 1))
                sp.dma_start(o_last[h].rearrange("v (h d) n -> (v h) (d n)", d=DIM),
                             mixed_halves[:, h].rearrange("p d s t -> p (d s t)")).then_inc(halves_stored[h], 16)

            def load_half(h):
                sp.wait_ge(halves_stored[h], 16)
                for c in range(CH):
                    sp.dma_start(half_view(oT, h, c), o_last[h, :, c * P:(c + 1) * P, :].rearrange("v p n -> p v n")
                                 ).then_inc(halves_loaded[h], 16)

            store_o(LAST - 1)
            load_o(LAST - 1)
            store_y(LAST - 2)
            store_half(0)
            store_half(1)
            sp.wait_ge(os_ready, LAST)
            load_half(0)
            load_half(1)
            for h in range(2):
                if h == 1:
                    store_y(LAST - 1)
                for c in range(CH):
                    sp.wait_ge(halves_added, CH * h + c + 1)
                    sp.dma_start(y_last[h, c], x_last[:, c, h * HALF_UNIT:(h + 1) * HALF_UNIT]).then_inc(y_last_stored, 16)
            for c in range(CH):
                sp.wait_ge(y_stored[c], 16 * LAST)
            sp.wait_ge(y_last_stored, 16 * 2 * CH)

        @block.tensor
        def _(pe):
            def sum_style(m):
                for c in range(CH):
                    last = pe.matmul(style_sum[:, m, c, :], affine[m][:, c * P:(c + 1) * P], cond, start=True, stop=True)
                last.then_inc(style_summed, 1)

            def sum_var(m):
                pe.wait_ge(style_squared, m + 1)
                pe.wait_ge(w_squared, m + 1)
                for c in range(CH):
                    for i in range(CH):
                        last = pe.matmul(var_sum[:, m, c, :], w_sq[:, m, i, c * P:(c + 1) * P], style_sq[:, m, i, :],
                                         start=(i == 0), stop=(i == CH - 1))
                last.then_inc(var_summed, 1)

            def project(u, c):
                pe.wait_ge(xs_ready, u + 1)
                for i in range(CH):
                    last = pe.matmul(proj[c][:], wT[:, 0, i, c * P:(c + 1) * P], xs[:, u % 2, i, :],
                                     start=(i == 0), stop=(i == CH - 1))
                last.then_inc(k_projected[c], 1)

            def finish(u, c):
                pe.wait_ge(os_ready, u + 1)
                for i in range(CH):
                    last = pe.matmul(proj[c][:], wT[:, 1, i, c * P:(c + 1) * P], os_[:, i, :],
                                     start=(i == 0), stop=(i == CH - 1))
                last.then_inc(y_projected[c], 1)

            def scores(u, h):
                pe.wait_ge(k_stat_ready, 2 * u + h + 1)
                pe.wait_ge(blocks1_ready, 2 * u + h + 1)
                if h == 1 or isinstance(u, int) and u == 0:
                    pe.wait_ge(blocks1_act, u + h + 1)
                wait_positive(pe, centered, 2 * u + h - 1)
                for t in range(HT):
                    for half in range(2):
                        for strip in range(4):
                            n = (h * HT + t) * PACK + 2 * strip + half
                            col = PAD + n * STRIP - half * PAD
                            last = pe.matmul(score[h][STRIP * strip:STRIP * (strip + 1), t], k_stat[:, col:col + STRIP],
                                             blocks1[:, :, n, :], start=(half == 0), stop=(half == 1))
                last.then_inc(scored, 1)

            def turn(u, h):
                pe.wait_ge(exp_ready, 2 * u + h + 1)
                wait_positive(pe, a_stat_ready, 2 * u + h - 1)
                for t in range(HT):
                    last = pe.transpose(turned[h][:, t].rearrange("p s h -> p (s h)"),
                                        attn[:, h, t].rearrange("p s j -> p (s j)"), ident)
                last.then_inc(attn_turned, 1)

            def mix_values(u, h):
                pe.wait_ge(a_stat_ready, 2 * u + h + 1)
                pe.wait_ge(blocks2_act, 2 * u + h + 1)
                pe.wait_ge(blocks2_pool, 2 * u + h + 1)
                for k in range(2):
                    g = 2 * h + k
                    wait_positive(pe, mix_divided, GROUPS * u + g - 1)
                    for t in range(2):
                        for half in range(2):
                            for strip in range(4):
                                n = (2 * g + t) * PACK + 2 * strip + half
                                col = PAD + n * STRIP - half * PAD
                                last = pe.matmul(mix[g % 2][STRIP * strip:STRIP * (strip + 1), t], a_stat[:, col:col + STRIP],
                                                 blocks2[:, :, n, :], start=(half == 0), stop=(half == 1))
                    last.then_inc(mix_done, 1)

            pe.wait_ge(params_loaded, 16)
            sum_style(0)
            sum_var(0)
            pe.wait_ge(weights_loaded[0], 16)
            for u in range(AHEAD):
                for c in range(CH):
                    wait_positive(pe, k_evacuated[c], u)
                    project(u, c)
                    if (u, c) == (0, 0):
                        pe.wait_ge(ident_loaded, 16)
                        sum_style(1)
                if u == 0:
                    sum_var(1)

            def unit(u, ahead=False):
                scores(u, 0)
                scores(u, 1)
                for c in range(CH):
                    if ahead:
                        pe.wait_ge(k_evacuated[c], u + AHEAD)
                        wait_positive(pe, y_evacuated[c], u - 1)
                        project(u + AHEAD, c)
                    else:
                        pe.wait_ge(k_evacuated[c], UNITS)
                        pe.wait_ge(y_evacuated[c], u - 2)
                        finish(u - 2, c)
                    turn(u, c)
                mix_values(u, 0)
                mix_values(u, 1)
                if ahead and 0 < u < PHASE - 1:
                    for c in range(CH):
                        pe.wait_ge(k_evacuated[c], u + AHEAD + 1)
                        wait_positive(pe, y_evacuated[c], u - 1)
                        finish(u - 1, c)

            for u in range(PHASE):
                unit(u, ahead=True)
            with pe.Fori(PHASE, UNITS) as u:
                unit(u)
            for c in range(CH):
                pe.wait_ge(y_evacuated[c], LAST - 1)
                finish(LAST - 1, c)
            for h in range(2):
                pe.wait_ge(halves_scaled, h + 1)
                for c in range(CH):
                    if h == 0:
                        pe.wait_ge(y_evacuated[c], LAST)
                    for i in range(CH):
                        last = pe.matmul(y_banks[h][c], wT[:, 1, i, c * P:(c + 1) * P],
                                         os_[:, i, h * HALF_UNIT:(h + 1) * HALF_UNIT],
                                         start=(i == 0), stop=(i == CH - 1))
                    last.then_inc(halves_finished, 1)

        @block.vector
        def _(dve):
            dve.memset(k_stat[:], 0.0).then_inc(pads_zeroed, 1)
            def styles(m):
                dve.wait_ge(style_summed, m + 1)
                for c in range(CH):
                    dve.tensor_scalar(style[:, m, c, :], style_sum[:, m, c, :], affine_bias[:, m, c:c + 1], None,
                                      ALU.add).then_inc(style_ready, 1)
                dve.wait_ge(style_ready, CH * (m + 1))
                dve.tensor_tensor(style_sq[:, m], style[:, m], style[:, m], ALU.mult).then_inc(style_squared, 1)

            def square_w(m):
                dve.wait_ge(weights_loaded[m], 16)
                dve.tensor_tensor(w_sq[:, m], wT[:, m], wT[:, m], ALU.mult).then_inc(w_squared, 1)

            def demodulation(m):
                dve.wait_ge(var_summed, m + 1)
                dve.tensor_scalar(var[:, m], var_sum[:, m], EPS, None, ALU.add).then_inc(var_ready, 1)
                dve.wait_ge(root_ready, m + 1)
                dve.reciprocal(inv0[:, m], root[:, m]).then_inc(demod_step, 1)
                dve.wait_ge(demod_step, 4 * m + 1)
                dve.tensor_tensor(newton[:, m], inv0[:, m], inv0[:, m], ALU.mult).then_inc(demod_step, 1)
                dve.wait_ge(demod_step, 4 * m + 2)
                dve.tensor_tensor(newton2[:, m], newton[:, m], var[:, m], ALU.mult).then_inc(demod_step, 1)
                dve.wait_ge(demod_step, 4 * m + 3)
                dve.tensor_scalar(newton[:, m], newton2[:, m], -0.5, 1.5, ALU.mult, ALU.add).then_inc(demod_step, 1)
                dve.wait_ge(demod_step, 4 * m + 4)
                dve.tensor_tensor(demod[:, m], newton[:, m], inv0[:, m], ALU.mult).then_inc(demod_ready, 1)

            def scale_x(u):
                for c in range(CH):
                    wait_positive(dve, k_projected[c], u - 1)
                dve.wait_ge(x_loaded[u], 16)
                for i in range(CH):
                    for b in range(BPU):
                        last = dve.tensor_scalar(xs[:, u % 2, i, b * SEQ:(b + 1) * SEQ], xT[:, u, i, b * SEQ:(b + 1) * SEQ],
                                                 style[:, 0, i, BPU * u + b:BPU * u + b + 1], None, ALU.mult)
                last.then_inc(xs_ready, 1)

            def spread_stat(u, h):
                dve.wait_ge(k_sd_loaded, PACK * 16 * (u + 1))
                wait_positive(dve, scored, 2 * u + h - 1)
                n0 = h * OCTETS // 2
                dve.tensor_copy(k_cols[:, n0:n0 + OCTETS // 2, :],
                                 k_sd[:, :, n0:n0 + OCTETS // 2].rearrange("p h n -> p n h")).then_inc(k_stat_ready, 1)

            def spread1(u, h, terms=PACK):
                dve.wait_ge(k_stat_ready, 2 * u + h + 1)
                wait_positive(dve, scored, 2 * u + h - 1)
                n0 = h * OCTETS // 2
                for s in range(terms):
                    last = dve.tensor_scalar(blocks1[:, s, n0:n0 + OCTETS // 2, :], k_cols[:, n0:n0 + OCTETS // 2, :],
                                             block_mask[:, s:s + 1], None, ALU.mult)
                last.then_inc(blocks1_ready, 1)

            def center(u, h):
                dve.wait_ge(scored, 2 * u + h + 1)
                dve.tensor_reduce(row_max[:, h], score[h][:], AX.X, ALU.max).then_inc(max_ready, 1)
                dve.wait_ge(max_ready, 2 * u + h + 1)
                wait_positive(dve, attn_turned, 2 * u + h - 1)
                dve.tensor_tensor(attn[:, h].rearrange("p t s j -> p (t s) j"), score[h][:].rearrange("p t s j -> p (t s) j"),
                                  row_max[:, h].rearrange("p t s -> p (t s)").unsqueeze(2).to_broadcast([P, HT * PACK, HEADS]),
                                  ALU.subtract).then_inc(centered, 1)

            def divide(u, g):
                dve.wait_ge(mix_done, GROUPS * u + g + 1)
                dve.reciprocal(inv_sum[:, g], mix[g % 2][:, :, :, DIM]).then_inc(inv_ready, 1)
                dve.wait_ge(inv_ready, GROUPS * u + g + 1)
                if g == 0:
                    wait_positive(dve, o_stored, 16 * u)
                tiles = (mixed_halves[:, g // 2, :, :, 2 * (g % 2):2 * (g % 2) + 2] if isinstance(u, int) and u == LAST
                         else mixed[:, :, :, 2 * g:2 * g + 2])
                dve.tensor_tensor(tiles.rearrange("p d s t -> p t s d"),
                                  mix[g % 2][:, :, :, 0:DIM],
                                  inv_sum[:, g].unsqueeze(3).to_broadcast([P, 2, PACK, DIM]),
                                  ALU.mult).then_inc(mix_divided, 1)

            def scale_o(u):
                dve.wait_ge(oT_loaded, CH * 16 * (u + 1))
                for c in range(CH):
                    wait_positive(dve, y_projected[c], u)
                for i in range(CH):
                    for b in range(BPU):
                        dst = os_[:, i, :].rearrange("p (v r) -> p v r", v=PACK)[:, :, b * OCTETS // 2:(b + 1) * OCTETS // 2]
                        src = oT[:, i, :].rearrange("p (v r) -> p v r", v=PACK)[:, :, b * OCTETS // 2:(b + 1) * OCTETS // 2]
                        last = dve.tensor_scalar(dst, src, style[:, 1, i, bass.ds(BPU * u + b, 1)], None, ALU.mult)
                last.then_inc(os_ready, 1)

            styles(0)
            square_w(0)
            scale_x(0)
            demodulation(0)
            scale_x(1)
            styles(1)
            square_w(1)
            demodulation(1)
            for u in range(2, AHEAD):
                scale_x(u)
            dve.wait_ge(blocks_zeroed, 1)
            for h in range(2):
                spread_stat(0, h)
                spread1(0, h, DVE_TERMS)
            scale_x(AHEAD)

            center(0, 0)
            center(0, 1)
            spread_stat(1, 0)
            spread_stat(1, 1)
            spread1(1, 0)
            divide(0, 0)
            divide(0, 1)
            spread1(1, 1, DVE_TERMS)
            divide(0, 2)
            divide(0, 3)
            scale_x(AHEAD + 1)

            def unit(u, ahead=False, spread=True):
                center(u, 0)
                center(u, 1)
                if spread:
                    spread_stat(u + 1, 0)
                    spread_stat(u + 1, 1)
                    spread1(u + 1, 0)
                divide(u, 0)
                divide(u, 1)
                if ahead or not spread:
                    scale_o(u - 1)
                else:
                    spread1(u + 1, 1, DVE_TERMS)
                divide(u, 2)
                divide(u, 3)
                if ahead:
                    spread1(u + 1, 1, DVE_TERMS)
                    scale_x(u + AHEAD + 1)
                elif spread:
                    scale_o(u - 1)

            for u in range(1, PHASE - 1):
                unit(u, ahead=True)
            with dve.Fori(PHASE - 1, LAST) as u:
                unit(u)
            unit(LAST, spread=False)

            for c in range(CH):
                dve.wait_ge(y_projected[c], LAST)
            for h in range(2):
                dve.wait_ge(halves_loaded[h], 16 * CH)
                for i in range(CH):
                    for b in range(BPU):
                        rows = slice(b * OCTETS // 4, (b + 1) * OCTETS // 4)
                        last = dve.tensor_scalar(half_view(os_, h, i)[:, :, rows], half_view(oT, h, i)[:, :, rows],
                                                 style[:, 1, i, BPU * LAST + b:BPU * LAST + b + 1], None, ALU.mult)
                last.then_inc(halves_scaled, 1)
            dve.wait_ge(x_biased, 2 * CH)
            for h in range(2):
                for c in range(CH):
                    dve.wait_ge(halves_finished, CH * h + c + 1)
                    for b in range(BPU):
                        rows = slice(b * OCTETS // 4, (b + 1) * OCTETS // 4)
                        last = dve.scalar_tensor_tensor(
                            half_view(x_last, h, c)[:, :, rows],
                            y_banks[h][c].rearrange("p (v n) -> p v n", v=PACK)[:, :, rows],
                            demod[:, 1, c, BPU * LAST + b:BPU * LAST + b + 1], half_view(x_last, h, c)[:, :, rows],
                            ALU.mult, ALU.add)
                    last.then_inc(halves_added, 1)

        @block.gpsimd
        def _(pool):
            pool.memset(blocks1[:], 0.0).then_inc(blocks_zeroed, 1)
            pool.memset(blocks2[:], 0.0).then_inc(blocks_zeroed, 1)
            pool.memset(a_stat[:], 0.0).then_inc(pads_zeroed, 1)
            pool.wait_ge(params_loaded, 16)
            pool.wait_ge(blocks_zeroed, 2)
            pool.wait_ge(pads_zeroed, 2)
            for s in range(PACK):
                pool.tensor_copy(blocks2[:, s, :, DIM], block_mask[:, s:s + 1].to_broadcast([P, OCTETS])
                                 ).then_inc(ones_set, 1)

            def spread2(u, h, terms=ACT_TERMS):
                pool.wait_ge(k_sj_copied, u + 1)
                wait_positive(pool, mix_done, GROUPS * u + 2 * h - 2)
                n0 = h * OCTETS // 2
                for s in range(terms, PACK):
                    last = pool.tensor_tensor(blocks2[:, s, n0:n0 + OCTETS // 2, 0:DIM],
                                              k_sjc[:, n0:n0 + OCTETS // 2, :],
                                              block_mask[:, s:s + 1].unsqueeze(2).to_broadcast([P, OCTETS // 2, DIM]),
                                              ALU.mult)
                last.then_inc(blocks2_pool, 1)

            def add_x(u):
                for c in range(CH):
                    pool.wait_ge(y_evacuated[c], u + 1)
                    y_view = yT[:, c, :].rearrange("p (v r) -> p v r", v=PACK)
                    pool.tensor_tensor(y_view, y_view, xT[:, u, c, :].rearrange("p (r v) -> p v r", v=PACK),
                                       ALU.add).then_inc(y_added[c], 1)

            spread2(0, 0)
            spread2(0, 1, ACT_TERMS_FIRST)

            def unit(u):
                spread2(u + 1, 0)
                spread2(u + 1, 1)

            for u in range(PHASE):
                unit(u)
                if 0 < u < PHASE - 1:
                    add_x(u - 1)
            with pool.Fori(PHASE, LAST) as u:
                add_x(u - 2)
                unit(u)
            add_x(LAST - 2)
            add_x(LAST - 1)

        @block.scalar
        def _(act):
            def roots(m):
                act.wait_ge(var_ready, m + 1)
                act.activation(root[:, m], var[:, m], ACT.Sqrt).then_inc(root_ready, 1)
                act.wait_ge(demod_ready, m + 1)

            def evacuate_k(u, c):
                act.wait_ge(k_projected[c], u + 1)
                wait_positive(act, k_stored[c], 16 * (u - AHEAD + 1))
                for b in range(BPU):
                    q = BPU * u + b
                    last = act.activation(kT[:, u % AHEAD, c, b * SEQ:(b + 1) * SEQ], proj[c][:, b * SEQ:(b + 1) * SEQ], ACT.Identity,
                                          bias=out_bias[:, 0, c:c + 1], scale=demod[:, 0, c, q:q + 1])
                last.then_inc(k_evacuated[c], 1)

            def exponent(u, h):
                act.wait_ge(centered, 2 * u + h + 1)
                act.activation(attn[:, h], attn[:, h], ACT.Exp, scale=SCALE).then_inc(exp_ready, 1)

            def copy_turned(u, h):
                act.wait_ge(attn_turned, 2 * u + h + 1)
                wait_positive(act, mix_done, GROUPS * u + 2 * h - 2)
                n0 = h * OCTETS // 2
                act.activation(a_cols[:, n0:n0 + OCTETS // 2, :], turned[h][:].rearrange("p t v h -> p (t v) h"),
                               ACT.Copy).then_inc(a_stat_ready, 1)

            def copy_sj(u):
                act.wait_ge(k_sj_loaded, 16 * (u + 1))
                wait_positive(act, blocks2_act, 2 * u)
                wait_positive(act, blocks2_pool, 2 * u)
                act.activation(k_sjc[:], k_sj[:].rearrange("p d n -> p n d"), ACT.Copy).then_inc(k_sj_copied, 1)

            def store_k(u, c):
                act.wait_ge(k_evacuated[c], u + 1)
                wait_positive(act, k_stored[c], 16 * u)
                act.dma_start(k_scratch[u, :, c * P:(c + 1) * P, :].rearrange("s p n -> p s n"),
                              kT[:, u % AHEAD, c, :].rearrange("p (s n) -> p s n", s=PACK)).then_inc(k_stored[c], 16)

            def spread2(u, h, terms=ACT_TERMS):
                act.wait_ge(k_sj_copied, u + 1)
                wait_positive(act, mix_done, GROUPS * u + 2 * h - 2)
                n0 = h * OCTETS // 2
                for s in range(terms):
                    last = act.activation(blocks2[:, s, n0:n0 + OCTETS // 2, 0:DIM],
                                          k_sjc[:, n0:n0 + OCTETS // 2, :],
                                          ACT.Copy, scale=block_mask[:, s:s + 1])
                last.then_inc(blocks2_act, 1)

            def evacuate_y(u, c):
                act.wait_ge(y_projected[c], u + 1)
                wait_positive(act, y_stored[c], 16 * u)
                for b in range(BPU):
                    q = BPU * u + b
                    half = slice(b * OCTETS // 2, (b + 1) * OCTETS // 2)
                    last = act.activation(yT[:, c, :].rearrange("p (v r) -> p v r", v=PACK)[:, :, half],
                                          proj[c][:].rearrange("p (v r) -> p v r", v=PACK)[:, :, half], ACT.Identity,
                                          bias=out_bias[:, 1, c:c + 1], scale=demod[:, 1, c, bass.ds(q, 1)])
                last.then_inc(y_evacuated[c], 1)

            def spread1_share(u, h):
                act.wait_ge(k_stat_ready, 2 * u + h + 1)
                wait_positive(act, scored, 2 * u + h - 1)
                n0 = h * OCTETS // 2
                for s in range(DVE_TERMS, PACK):
                    last = act.activation(blocks1[:, s, n0:n0 + OCTETS // 2, :], k_cols[:, n0:n0 + OCTETS // 2, :],
                                          ACT.Copy, scale=block_mask[:, s:s + 1])
                last.then_inc(blocks1_act, 1)

            roots(0)
            for c in range(CH):
                evacuate_k(0, c)
                store_k(0, c)
            roots(1)
            evacuate_k(1, 0)
            store_k(1, 0)
            evacuate_k(1, 1)
            act.activation(root[:], demod[:], ACT.Exp)
            for u in (2, 3):
                for c in range(CH):
                    evacuate_k(u, c)
            act.wait_ge(k_sd_loaded, PACK * 16)
            store_k(1, 1)
            act.wait_ge(blocks_zeroed, 1)
            spread1_share(0, 0)
            copy_sj(0)
            spread1_share(0, 1)
            for c in range(CH):
                evacuate_k(4, c)
            act.wait_ge(pads_zeroed, 2)
            act.wait_ge(ones_set, PACK)

            def unit(u, ahead=False, spread=True):
                exponent(u, 0)
                if ahead and u == 0:
                    spread2(0, 0)
                    for c in range(CH):
                        store_k(2, c)
                exponent(u, 1)
                for c in range(CH):
                    if ahead:
                        evacuate_k(u + AHEAD, c)
                    else:
                        evacuate_y(u - 2, c)
                    copy_turned(u, c)
                if ahead and u == 0:
                    spread2(0, 1, ACT_TERMS_FIRST)
                if spread:
                    spread1_share(u + 1, 1)
                if ahead:
                    for c in range(CH):
                        store_k(2 * u + 2 if u > 0 else 3, c)
                if spread:
                    copy_sj(u + 1)
                    spread2(u + 1, 0)
                    spread2(u + 1, 1)
                if ahead and u > 0:
                    for c in range(CH):
                        store_k(2 * u + 3, c)
                if ahead and 0 < u < PHASE - 1:
                    for c in range(CH):
                        evacuate_y(u - 1, c)

            for u in range(PHASE):
                unit(u, ahead=True)
            with act.Fori(PHASE, LAST) as u:
                unit(u)
            unit(LAST, spread=False)
            act.wait_ge(x_loaded[LAST], 16)
            for h in range(2):
                for c in range(CH):
                    act.activation(half_view(x_last, h, c).rearrange("p v (s t) -> p s t v", s=PACK),
                                   xT[:, LAST, c, :].rearrange("p (s a t v) -> p a s t v", s=PACK, a=2, v=PACK)[:, h],
                                   ACT.Identity, bias=out_bias[:, 1, c:c + 1]).then_inc(x_biased, 1)
            for c in range(CH):
                evacuate_y(LAST - 1, c)


def kernel(x, cond_512, L0_cond_k_aff_w, L0_cond_k_aff_b, L0_cond_k_w, L0_cond_k_b,
           L0_cond_o_aff_w, L0_cond_o_aff_b, L0_cond_o_w, L0_cond_o_b):
    import numpy as np
    import concourse.bacc as bacc
    from concourse.bass_utils import run_bass_kernel_spmd

    fp32 = mybir.dt.float32
    x_in = np.ascontiguousarray(np.asarray(x).reshape(UNITS, UNIT, CH, P).transpose(0, 2, 3, 1))

    def column(v):
        return np.asarray(v).reshape(CH, P).T

    mask = np.repeat(np.eye(PACK, dtype=np.float32), DIM, axis=0)
    params = np.ascontiguousarray(np.concatenate([
        np.asarray(L0_cond_k_aff_w).T, np.asarray(cond_512).T,
        column(L0_cond_k_aff_b), column(L0_cond_o_aff_b), column(L0_cond_k_b), column(L0_cond_o_b),
        mask, np.asarray(L0_cond_o_aff_w).T, np.eye(P, dtype=np.float32)], axis=1))
    weights = np.ascontiguousarray(np.stack([np.asarray(L0_cond_k_w).T, np.asarray(L0_cond_o_w).T]))

    nc = bacc.Bacc("TRN2", target_bir_lowering=False, num_devices=1)
    arrays = {"x_in": x_in, "params": params, "weights": weights}
    aps = [nc.dram_tensor(name, a.shape, fp32, kind="ExternalInput").ap() for name, a in arrays.items()]
    y = nc.dram_tensor("y", (LAST, CH, P, UNIT), fp32, kind="ExternalOutput").ap()
    y_last = nc.dram_tensor("y_last", (2, CH, P, HALF_UNIT), fp32, kind="ExternalOutput").ap()
    build(nc, *aps, y, y_last)
    result = run_bass_kernel_spmd(nc, [arrays], core_ids=[0])
    out = result.results[0]["y"].reshape(LAST, FEAT, PACK, PACK, TILES).transpose(0, 3, 4, 2, 1)
    last = result.results[0]["y_last"].reshape(2, FEAT, PACK, PACK, HT).transpose(3, 0, 4, 2, 1)
    return np.concatenate([out.reshape(-1, FEAT), last.reshape(-1, FEAT)]).reshape(BATCH, SEQ, FEAT)
```

```python
from contextlib import ExitStack

import concourse.bass as bass
from concourse import mybir

BATCH, SEQ, FEAT, HEADS = 16, 256, 256, 16
DIM = FEAT // HEADS
P = 128
UNIT = 512
UNITS = BATCH * SEQ // UNIT
HALF_UNIT = UNIT // 2
BPU = UNIT // SEQ
CH = FEAT // P
PACK = P // DIM
OCTETS = UNIT // PACK
TILES = OCTETS // PACK
HT = TILES // 2
GROUPS = 4
STRIP = 32
PAD = DIM
DE = DIM + 1
EARLY_X = 7
AHEAD = 5
PHASE = UNITS - AHEAD
LAST = UNITS - 1
EPS = 1e-8
SCALE = 1.0 / float(DIM) ** 0.5
DVE_TERMS = (7, 5)
ACT_TERMS = 1
SIDES = 2
FOUR = PACK // SIDES


def wait_positive(engine, semaphore, value):
    if not isinstance(value, int) or value > 0:
        engine.wait_ge(semaphore, value)


def build(nc, x, params, weights, y, y_last):
    fp32 = mybir.dt.float32
    ALU = mybir.AluOpType
    ACT = mybir.ActivationFunctionType
    AX = mybir.AxisListType

    k_scratch = nc.dram_tensor("k_scratch", (UNITS, PACK, FEAT, OCTETS), fp32, kind="Internal").ap()
    o_scratch = nc.dram_tensor("o_scratch", (UNITS, PACK, FEAT, OCTETS), fp32, kind="Internal").ap()
    o_last = nc.dram_tensor("o_last", (2, PACK, FEAT, OCTETS // 2), fp32, kind="Internal").ap()

    ctx = ExitStack()
    with ctx:
        def sb(name, shape):
            return ctx.enter_context(nc.sbuf_tensor(name, shape, fp32))

        def pb(name, shape):
            return ctx.enter_context(nc.psum_tensor(name, shape, fp32))

        def sem(name):
            return ctx.enter_context(nc.semaphore(name))

        head = FEAT + BATCH + 2 * 2 * CH + PACK + FOUR
        par = sb("par", [P, params.shape[1]])
        affine = [par[:, 0:FEAT], par[:, head:head + FEAT]]
        cond = par[:, FEAT:FEAT + BATCH]
        at = FEAT + BATCH
        affine_bias = par[:, at:at + 4].rearrange("p (m c) -> p m c", m=2)
        out_bias = par[:, at + 4:at + 8].rearrange("p (m c) -> p m c", m=2)
        block_mask = par[:, at + 8:at + 8 + PACK]
        four_mask = par[:, at + 8 + PACK:head]
        ident = par[:, head + FEAT:head + FEAT + P]
        wT = sb("wT", [P, 2, CH, FEAT])
        w_sq = sb("w_sq", [P, 2, CH, FEAT])
        style = sb("style", [P, 2, CH, BATCH])
        style_sq = sb("style_sq", [P, 2, CH, BATCH])
        var = sb("var", [P, 2, CH, BATCH])
        root = sb("root", [P, 2, CH, BATCH])
        inv0 = sb("inv0", [P, 2, CH, BATCH])
        newton = sb("newton", [P, 2, CH, BATCH])
        newton2 = sb("newton2", [P, 2, CH, BATCH])
        demod = sb("demod", [P, 2, CH, BATCH])

        unread = sb("unread", [P, 1])

        xT = sb("xT", [P, UNITS, CH, UNIT])
        xs = sb("xs", [P, 2, CH, UNIT])
        kT = sb("kT", [P, AHEAD, CH, UNIT])
        k_sd = sb("k_sd", [P, HEADS, OCTETS])
        k_sj = sb("k_sj", [P, DIM, OCTETS])
        k_stat = sb("k_stat", [P, PAD + OCTETS * STRIP])
        blocks1 = sb("blocks1", [P, PACK, OCTETS, HEADS])
        blocks2 = sb("blocks2", [P, FOUR, OCTETS, DE])
        row_max = sb("row_max", [P, 2, HT, PACK])
        attn = sb("attn", [P, 2, HT, PACK, HEADS])
        k_sjc = sb("k_sjc", [P, OCTETS, DIM])
        a_stat = sb("a_stat", [P, OCTETS, SIDES, HEADS])
        inv_sum = sb("inv_sum", [P, GROUPS, FOUR, FOUR])
        mixed = sb("mixed", [P, DIM, FOUR, 2 * TILES])
        oT = sb("oT", [P, CH, UNIT])
        os_ = sb("os", [P, CH, UNIT])
        yT = sb("yT", [P, CH, UNIT])
        x_last = sb("x_last", [P, CH, UNIT])

        proj = [pb(f"proj{c}", [P, UNIT]) for c in range(CH)]
        score = [pb(f"score{h}", [P, HT, PACK, HEADS]) for h in range(2)]
        turned = [pb(f"turned{h}", [P, HT, PACK, HEADS]) for h in range(2)]
        mix = [pb(f"mix{g}", [P, FOUR, FOUR, DE])[:] for g in range(2)]
        mix += [turned[h][:].rearrange("p t v h -> p (t v h)")[:, 0:FOUR * FOUR * DE].rearrange(
            "p (t s d) -> p t s d", t=FOUR, s=FOUR) for h in range(2)]

        mixed_halves = mixed[:].rearrange("p d s t -> p (d s t)").rearrange("p (a d s t) -> p a d s t", a=2, d=DIM, s=FOUR)
        y_banks = [[proj[c][:, 0:HALF_UNIT] for c in range(CH)],
                   [score[c][:].rearrange("p t s j -> p (t s j)")[:, 0:HALF_UNIT] for c in range(CH)]]

        def half_view(buffer, h, c):
            return buffer[:, c, h * HALF_UNIT:(h + 1) * HALF_UNIT].rearrange("p (v n) -> p v n", v=PACK)

        def of_batch(tokens, b):
            return tokens.rearrange("p (c g r) -> p c g r", c=FOUR, g=SIDES)[:, :, b, :]

        os_last = xs[:, 0]

        style_sum = turned[0][:, 0].rearrange("p s h -> p (s h)")[:, 0:2 * CH * BATCH].rearrange(
            "p (m c b) -> p m c b", m=2, c=CH)
        var_sum = turned[1][:, 0].rearrange("p s h -> p (s h)")[:, 0:2 * CH * BATCH].rearrange(
            "p (m c b) -> p m c b", m=2, c=CH)

        k_cols = k_stat[:, PAD:].rearrange("p (n w) -> p n w", w=STRIP)[:, :, 0:HEADS]

        params_loaded, ident_loaded = sem("params_loaded"), sem("ident_loaded")
        weights_loaded = [sem(f"weights_loaded{m}") for m in range(2)]
        x_loaded = [sem(f"x_loaded{u}") for u in range(UNITS)]
        style_summed, style_ready, style_squared = sem("style_summed"), sem("style_ready"), sem("style_squared")
        w_squared, var_summed, var_ready = sem("w_squared"), sem("var_summed"), sem("var_ready")
        root_ready, demod_step, demod_ready = sem("root_ready"), sem("demod_step"), sem("demod_ready")
        pads_zeroed, blocks_zeroed, ones_set = sem("pads_zeroed"), sem("blocks_zeroed"), sem("ones_set")
        xs_ready = sem("xs_ready")
        k_projected = [sem(f"k_projected{c}") for c in range(CH)]
        k_evacuated = [sem(f"k_evacuated{c}") for c in range(CH)]
        k_stored = [sem(f"k_stored{c}") for c in range(CH)]
        k_sd_loaded, k_sj_loaded = sem("k_sd_loaded"), sem("k_sj_loaded")
        k_stat_ready, blocks1_ready = sem("k_stat_ready"), sem("blocks1_ready")
        blocks1_act = sem("blocks1_act")
        k_sj_copied = sem("k_sj_copied")
        blocks2_act, blocks2_pool = sem("blocks2_act"), sem("blocks2_pool")
        scored, max_ready, centered, exp_ready = sem("scored"), sem("max_ready"), sem("centered"), sem("exp_ready")
        attn_turned, a_stat_ready = sem("attn_turned"), sem("a_stat_ready")
        mix_done, inv_ready, mix_divided = sem("mix_done"), sem("inv_ready"), sem("mix_divided")
        o_stored, oT_loaded, os_ready = sem("o_stored"), sem("oT_loaded"), sem("os_ready")
        y_projected = [sem(f"y_projected{c}") for c in range(CH)]
        y_evacuated = [sem(f"y_evacuated{c}") for c in range(CH)]
        y_added = [sem(f"y_added{c}") for c in range(CH)]
        y_stored = [sem(f"y_stored{c}") for c in range(CH)]

        halves_stored = [sem(f"half{h}_stored") for h in range(2)]
        halves_loaded = [[sem(f"half{h}_loaded{c}") for c in range(CH)] for h in range(2)]
        x_biased, halves_scaled, halves_finished = sem("x_biased"), sem("halves_scaled"), sem("halves_finished")
        halves_added, y_last_stored = sem("halves_added"), sem("y_last_stored")

        block = ctx.enter_context(nc.Block())

        @block.sync
        def _(sp):
            sp.dma_start(par[:, 0:head], params[:, 0:head]).then_inc(params_loaded, 16)

            def load_w(m):
                sp.dma_start(wT[:, m], weights[m].rearrange("(c p) o -> p c o", p=P)).then_inc(weights_loaded[m], 16)

            def counts(u):
                values = (u, u + 1, 2 * u, GROUPS * (u + 1), 16 * (u + 1))
                return values if isinstance(u, int) else tuple(sp.snap(sp.to_reg(v)) for v in values)

            def load_x(u):
                sp.dma_start(xT[:, u], x[u].rearrange("c p t -> p c t")).then_inc(x_loaded[u], 16)

            def load_sd(u):
                u, _, halves, _, dmas = counts(u)
                for c in range(CH):
                    sp.wait_ge(k_stored[c], dmas)
                wait_positive(sp, k_stat_ready, halves)
                for s in range(PACK):
                    sp.dma_start(k_sd[DIM * s:DIM * (s + 1)],
                                 k_scratch[u, s].rearrange("(h d) n -> d h n", d=DIM)).then_inc(k_sd_loaded, 16)

            def load_sj(u):
                u, _, _, _, dmas = counts(u)
                for c in range(CH):
                    sp.wait_ge(k_stored[c], dmas)
                wait_positive(sp, k_sj_copied, u)
                sp.dma_start(k_sj[:].rearrange("p d n -> p (d n)"),
                             k_scratch[u].rearrange("s (j d) n -> (s j) (d n)", d=DIM)).then_inc(k_sj_loaded, 16)

            def store_o(u):
                u, _, _, groups, _ = counts(u)
                sp.wait_ge(mix_divided, groups)
                sp.dma_start(o_scratch[u].rearrange("v (h d) n -> (v h) (d n)", d=DIM),
                             mixed[:].rearrange("p d s t -> p (d s t)")).then_inc(o_stored, 16)

            def load_o(u):
                u, _, _, _, dmas = counts(u)
                sp.wait_ge(o_stored, dmas)
                wait_positive(sp, os_ready, u)
                for c in range(CH):
                    sp.dma_start(oT[:, c, :].rearrange("p (v n) -> p v n", v=PACK),
                                 o_scratch[u, :, c * P:(c + 1) * P, :].rearrange("v p n -> p v n")
                                 ).then_inc(oT_loaded, 16)

            def store_y(u):
                u, next_u, _, _, _ = counts(u)
                for c in range(CH):
                    sp.wait_ge(y_added[c], next_u)
                    sp.dma_start(y[u, c], yT[:, c, :]).then_inc(y_stored[c], 16)

            load_w(0)
            load_x(0)
            sp.dma_start(par[:, head:], params[:, head:]).then_inc(ident_loaded, 16)
            load_x(1)
            load_w(1)
            load_x(2)
            load_x(3)
            load_x(4)
            load_x(5)
            load_sd(0)
            load_sj(0)
            load_sd(1)
            load_sj(1)
            load_x(6)
            load_sd(2)

            def unit(u, sd=True):
                store_o(u - 1)
                load_sj(u + 1)
                load_o(u - 1)
                if isinstance(u, int) and u + EARLY_X - 1 < UNITS:
                    load_x(u + EARLY_X - 1)
                if sd:
                    load_sd(u + 2)
                if not isinstance(u, int) or u > 1:
                    store_y(u - 2)

            for u in range(1, UNITS - EARLY_X + 1):
                unit(u)
            with sp.Fori(UNITS - EARLY_X + 1, LAST - 1) as u:
                unit(u)
            unit(LAST - 1, sd=False)

            def store_half(h):
                sp.wait_ge(mix_divided, GROUPS * LAST + 2 * (h + 1))
                sp.dma_start(o_last[h].rearrange("v (h d) n -> (v h) (d n)", d=DIM),
                             mixed_halves[:, h].rearrange("p d s t -> p (d s t)")).then_inc(halves_stored[h], 16)

            def load_half(h):
                sp.wait_ge(halves_stored[h], 16)
                for c in range(CH):
                    sp.dma_start(half_view(oT, h, c), o_last[h, :, c * P:(c + 1) * P, :].rearrange("v p n -> p v n")
                                 ).then_inc(halves_loaded[h][c], 16)

            store_o(LAST - 1)
            load_o(LAST - 1)
            store_half(0)
            store_half(1)
            sp.wait_ge(os_ready, LAST)
            load_half(0)
            load_half(1)
            for h in range(2):
                for c in range(CH):
                    sp.wait_ge(halves_added, CH * h + c + 1)
                    sp.dma_start(y_last[h, c], x_last[:, c, h * HALF_UNIT:(h + 1) * HALF_UNIT]).then_inc(y_last_stored, 16)
            for c in range(CH):
                sp.wait_ge(y_stored[c], 16 * LAST)
            sp.wait_ge(y_last_stored, 16 * 2 * CH)

        @block.tensor
        def _(pe):
            def sum_style(m):
                for c in range(CH):
                    last = pe.matmul(style_sum[:, m, c, :], affine[m][:, c * P:(c + 1) * P], cond, start=True, stop=True)
                last.then_inc(style_summed, 1)

            def sum_var(m):
                pe.wait_ge(style_squared, m + 1)
                pe.wait_ge(w_squared, m + 1)
                for c in range(CH):
                    for i in range(CH):
                        last = pe.matmul(var_sum[:, m, c, :], w_sq[:, m, i, c * P:(c + 1) * P], style_sq[:, m, i, :],
                                         start=(i == 0), stop=(i == CH - 1))
                last.then_inc(var_summed, 1)

            def project(u, c):
                pe.wait_ge(xs_ready, u + 1)
                for i in range(CH):
                    last = pe.matmul(proj[c][:], wT[:, 0, i, c * P:(c + 1) * P], xs[:, u % 2, i, :],
                                     start=(i == 0), stop=(i == CH - 1))
                last.then_inc(k_projected[c], 1)

            def finish(u, c):
                pe.wait_ge(os_ready, u + 1)
                for i in range(CH):
                    last = pe.matmul(proj[c][:], wT[:, 1, i, c * P:(c + 1) * P], os_[:, i, :],
                                     start=(i == 0), stop=(i == CH - 1))
                last.then_inc(y_projected[c], 1)

            def scores(u, h):
                pe.wait_ge(k_stat_ready, 2 * u + h + 1)
                pe.wait_ge(blocks1_ready, 2 * u + h + 1)
                pe.wait_ge(blocks1_act, 2 * u + h + 1)
                wait_positive(pe, centered, 2 * u + h - 1)
                for t in range(HT):
                    for half in range(2):
                        for strip in range(4):
                            n = (h * HT + t) * PACK + 2 * strip + half
                            col = PAD + n * STRIP - half * PAD
                            last = pe.matmul(score[h][STRIP * strip:STRIP * (strip + 1), t], k_stat[:, col:col + STRIP],
                                             blocks1[:, :, n, :], start=(half == 0), stop=(half == 1))
                last.then_inc(scored, 1)

            def turn(u, h):
                pe.wait_ge(exp_ready, 2 * u + h + 1)
                if not isinstance(u, int) or u > 0:
                    pe.wait_ge(mix_divided, GROUPS * (u - 1) + 2 + h + 1)
                for t in range(HT):
                    last = pe.transpose(turned[h][:, t].rearrange("p s h -> p (s h)"),
                                        attn[:, h, t].rearrange("p s j -> p (s j)"), ident)
                last.then_inc(attn_turned, 1)

            def mix_values(u, h):
                pe.wait_ge(a_stat_ready, 2 * u + h + 1)
                if not isinstance(u, int) or u > 0:
                    pe.wait_ge(blocks2_act, 2 * (u - 1) + h + 1)
                pe.wait_ge(blocks2_pool, 2 * u + h + 1)
                for k in range(2):
                    g = 2 * h + k
                    if g < 2:
                        wait_positive(pe, mix_divided, GROUPS * (u - 1) + g + 1)
                    for t in range(2):
                        for hi in range(2):
                            for strip in range(4):
                                n = (2 * g + t) * PACK + 4 * hi + strip
                                last = pe.matmul(mix[g][STRIP * strip:STRIP * (strip + 1), 2 * t + hi],
                                                 a_stat[:, n].rearrange("p g h -> p (g h)"), blocks2[:, :, n, :],
                                                 start=True, stop=True)
                    last.then_inc(mix_done, 1)

            pe.wait_ge(params_loaded, 16)
            sum_style(0)
            sum_var(0)
            pe.wait_ge(weights_loaded[0], 16)
            for u in range(AHEAD):
                for c in range(CH):
                    wait_positive(pe, k_evacuated[c], u)
                    project(u, c)
                    if (u, c) == (0, 0):
                        pe.wait_ge(ident_loaded, 16)
                        sum_style(1)
                if u == 0:
                    sum_var(1)

            def unit(u, ahead=False):
                scores(u, 0)
                if ahead and u > 1:
                    for c in range(CH):
                        pe.wait_ge(k_evacuated[c], u + AHEAD)
                        wait_positive(pe, y_evacuated[c], u - 2)
                        finish(u - 2, c)
                scores(u, 1)
                for c in range(CH):
                    if ahead:
                        pe.wait_ge(k_evacuated[c], u + AHEAD)
                        wait_positive(pe, y_evacuated[c], u - 1)
                        project(u + AHEAD, c)
                    else:
                        pe.wait_ge(k_evacuated[c], UNITS)
                        pe.wait_ge(y_evacuated[c], u - 2)
                        finish(u - 2, c)
                    turn(u, c)
                mix_values(u, 0)
                mix_values(u, 1)

            for u in range(PHASE):
                unit(u, ahead=True)
            with pe.Fori(PHASE, UNITS) as u:
                unit(u)
            for c in range(CH):
                pe.wait_ge(y_evacuated[c], LAST - 1)
                finish(LAST - 1, c)
            for h in range(2):
                for i in range(CH):
                    pe.wait_ge(halves_scaled, CH * h + i + 1)
                    for c in range(CH):
                        if h == 0 and i == 0:
                            pe.wait_ge(y_evacuated[c], LAST)
                        last = pe.matmul(y_banks[h][c], wT[:, 1, i, c * P:(c + 1) * P],
                                         os_last[:, i, h * HALF_UNIT:(h + 1) * HALF_UNIT],
                                         start=(i == 0), stop=(i == CH - 1))
                        if i == CH - 1:
                            last.then_inc(halves_finished, 1)

        @block.vector
        def _(dve):
            dve.memset(k_stat[:], 0.0).then_inc(pads_zeroed, 1)

            def styles(m):
                dve.wait_ge(style_summed, m + 1)
                for c in range(CH):
                    dve.tensor_scalar(style[:, m, c, :], style_sum[:, m, c, :], affine_bias[:, m, c:c + 1], None,
                                      ALU.add).then_inc(style_ready, 1)
                dve.wait_ge(style_ready, CH * (m + 1))
                dve.tensor_tensor(style_sq[:, m], style[:, m], style[:, m], ALU.mult).then_inc(style_squared, 1)

            def square_w(m):
                dve.wait_ge(weights_loaded[m], 16)
                dve.tensor_tensor(w_sq[:, m], wT[:, m], wT[:, m], ALU.mult).then_inc(w_squared, 1)

            def demodulation(m):
                dve.wait_ge(var_summed, m + 1)
                dve.tensor_scalar(var[:, m], var_sum[:, m], EPS, None, ALU.add).then_inc(var_ready, 1)
                dve.wait_ge(root_ready, m + 1)
                dve.reciprocal(inv0[:, m], root[:, m]).then_inc(demod_step, 1)
                dve.wait_ge(demod_step, 4 * m + 1)
                dve.tensor_tensor(newton[:, m], inv0[:, m], inv0[:, m], ALU.mult).then_inc(demod_step, 1)
                dve.wait_ge(demod_step, 4 * m + 2)
                dve.tensor_tensor(newton2[:, m], newton[:, m], var[:, m], ALU.mult).then_inc(demod_step, 1)
                dve.wait_ge(demod_step, 4 * m + 3)
                dve.tensor_scalar(newton[:, m], newton2[:, m], -0.5, 1.5, ALU.mult, ALU.add).then_inc(demod_step, 1)
                dve.wait_ge(demod_step, 4 * m + 4)
                dve.tensor_tensor(demod[:, m], newton[:, m], inv0[:, m], ALU.mult).then_inc(demod_ready, 1)

            def scale_x(u):
                for c in range(CH):
                    wait_positive(dve, k_projected[c], u - 1)
                dve.wait_ge(x_loaded[u], 16)
                for i in range(CH):
                    for b in range(BPU):
                        last = dve.tensor_scalar(xs[:, u % 2, i, b * SEQ:(b + 1) * SEQ], xT[:, u, i, b * SEQ:(b + 1) * SEQ],
                                                 style[:, 0, i, BPU * u + b:BPU * u + b + 1], None, ALU.mult)
                last.then_inc(xs_ready, 1)

            def spread_stat(u, h):
                dve.wait_ge(k_sd_loaded, PACK * 16 * (u + 1))
                wait_positive(dve, scored, 2 * u + h - 1)
                n0 = h * OCTETS // 2
                dve.tensor_copy(k_cols[:, n0:n0 + OCTETS // 2, :],
                                 k_sd[:, :, n0:n0 + OCTETS // 2].rearrange("p h n -> p n h")).then_inc(k_stat_ready, 1)

            def spread1(u, h):
                dve.wait_ge(k_stat_ready, 2 * u + h + 1)
                wait_positive(dve, scored, 2 * u + h - 1)
                n0 = h * OCTETS // 2
                for s in range(DVE_TERMS[h]):
                    last = dve.tensor_scalar(blocks1[:, s, n0:n0 + OCTETS // 2, :], k_cols[:, n0:n0 + OCTETS // 2, :],
                                             block_mask[:, s:s + 1], None, ALU.mult)
                last.then_inc(blocks1_ready, 1)

            def center(u, h):
                dve.wait_ge(scored, 2 * u + h + 1)
                dve.tensor_reduce(row_max[:, h], score[h][:], AX.X, ALU.max).then_inc(max_ready, 1)
                dve.wait_ge(max_ready, 2 * u + h + 1)
                wait_positive(dve, attn_turned, 2 * u + h - 1)
                dve.tensor_tensor(attn[:, h].rearrange("p t s j -> p (t s) j"), score[h][:].rearrange("p t s j -> p (t s) j"),
                                  row_max[:, h].rearrange("p t s -> p (t s)").unsqueeze(2).to_broadcast([P, HT * PACK, HEADS]),
                                  ALU.subtract).then_inc(centered, 1)

            def divide(u, h):
                pair = (2 * h, 2 * h + 1)
                for g in pair:
                    dve.wait_ge(mix_done, GROUPS * u + g + 1)
                    dve.reciprocal(inv_sum[:, g], mix[g][:, :, :, DIM]).then_inc(inv_ready, 1)
                if h == 0:
                    wait_positive(dve, o_stored, 16 * u)
                for g in pair:
                    dve.wait_ge(inv_ready, GROUPS * u + g + 1)
                    tiles = (mixed_halves[:, h, :, :, FOUR * (g % 2):FOUR * (g % 2 + 1)] if isinstance(u, int) and u == LAST
                             else mixed[:, :, :, FOUR * g:FOUR * (g + 1)])
                    dve.tensor_tensor(tiles.rearrange("p d s t -> p t s d"),
                                      mix[g][:, :, :, 0:DIM],
                                      inv_sum[:, g].unsqueeze(3).to_broadcast([P, FOUR, FOUR, DIM]),
                                      ALU.mult).then_inc(mix_divided, 1)

            def scale_o(u):
                dve.wait_ge(oT_loaded, CH * 16 * (u + 1))
                for c in range(CH):
                    wait_positive(dve, y_projected[c], u)
                for i in range(CH):
                    for b in range(BPU):
                        last = dve.tensor_scalar(of_batch(os_[:, i, :], b), of_batch(oT[:, i, :], b),
                                                 style[:, 1, i, bass.ds(BPU * u + b, 1)], None, ALU.mult)
                last.then_inc(os_ready, 1)

            styles(0)
            square_w(0)
            scale_x(0)
            demodulation(0)
            scale_x(1)
            styles(1)
            square_w(1)
            demodulation(1)
            for u in range(2, AHEAD):
                scale_x(u)
            dve.wait_ge(blocks_zeroed, 1)
            for h in range(2):
                spread_stat(0, h)
                spread1(0, h)
            scale_x(AHEAD)

            center(0, 0)
            center(0, 1)
            spread_stat(1, 0)
            spread_stat(1, 1)
            spread1(1, 0)
            divide(0, 0)
            spread1(1, 1)
            divide(0, 1)
            scale_x(AHEAD + 1)

            def unit(u, ahead=False, spread=True):
                center(u, 0)
                center(u, 1)
                if spread:
                    spread_stat(u + 1, 0)
                    spread_stat(u + 1, 1)
                    spread1(u + 1, 0)
                divide(u, 0)
                if ahead or not spread:
                    scale_o(u - 1)
                else:
                    spread1(u + 1, 1)
                divide(u, 1)
                if ahead:
                    spread1(u + 1, 1)
                    scale_x(u + AHEAD + 1)
                elif spread:
                    scale_o(u - 1)

            for u in range(1, PHASE - 1):
                unit(u, ahead=True)
            with dve.Fori(PHASE - 1, LAST) as u:
                unit(u)
            unit(LAST, spread=False)

            for h in range(2):
                for i in range(CH):
                    dve.wait_ge(halves_loaded[h][i], 16)
                    for b in range(BPU):
                        half = slice(h * HALF_UNIT, (h + 1) * HALF_UNIT)
                        last = dve.tensor_scalar(of_batch(os_last[:, i, half], b), of_batch(oT[:, i, half], b),
                                                 style[:, 1, i, BPU * LAST + b:BPU * LAST + b + 1], None, ALU.mult)
                    last.then_inc(halves_scaled, 1)
            dve.wait_ge(x_biased, 2 * CH)
            for h in range(2):
                for c in range(CH):
                    dve.wait_ge(halves_finished, CH * h + c + 1)
                    for b in range(BPU):
                        xy = of_batch(x_last[:, c, h * HALF_UNIT:(h + 1) * HALF_UNIT], b)
                        last = dve.scalar_tensor_tensor(
                            xy, of_batch(y_banks[h][c], b), demod[:, 1, c, BPU * LAST + b:BPU * LAST + b + 1], xy,
                            ALU.mult, ALU.add)
                    last.then_inc(halves_added, 1)

        @block.gpsimd
        def _(pool):
            pool.memset(blocks1[:], 0.0).then_inc(blocks_zeroed, 1)
            pool.memset(blocks2[:], 0.0).then_inc(blocks_zeroed, 1)
            pool.memset(a_stat[:], 0.0).then_inc(pads_zeroed, 1)
            pool.wait_ge(params_loaded, 16)
            pool.wait_ge(blocks_zeroed, 2)
            pool.wait_ge(pads_zeroed, 2)
            for s in range(FOUR):
                pool.tensor_copy(blocks2[:, s, :, DIM], four_mask[:, s:s + 1].to_broadcast([P, OCTETS])
                                 ).then_inc(ones_set, 1)

            def spread2(u, h):
                pool.wait_ge(k_sj_copied, u + 1)
                wait_positive(pool, mix_done, GROUPS * u + 2 * h - 2)
                n0 = h * OCTETS // 2
                for s in range(0 if isinstance(u, int) and u == 0 else ACT_TERMS, FOUR):
                    last = pool.tensor_tensor(blocks2[:, s, n0:n0 + OCTETS // 2, 0:DIM],
                                              k_sjc[:, n0:n0 + OCTETS // 2, :],
                                              four_mask[:, s:s + 1].unsqueeze(2).to_broadcast([P, OCTETS // 2, DIM]),
                                              ALU.mult)
                last.then_inc(blocks2_pool, 1)

            def add_x(u):
                for c in range(CH):
                    pool.wait_ge(y_evacuated[c], u + 1)
                    y_view = yT[:, c, :].rearrange("p (c r) -> p c r", c=FOUR)
                    pool.tensor_tensor(y_view, y_view, xT[:, u, c, :].rearrange("p (r c) -> p c r", c=FOUR),
                                       ALU.add).then_inc(y_added[c], 1)

            spread2(0, 0)
            spread2(0, 1)

            def unit(u):
                spread2(u + 1, 0)
                spread2(u + 1, 1)

            for u in range(PHASE):
                unit(u)
                if 0 < u < PHASE - 1:
                    add_x(u - 1)
            with pool.Fori(PHASE, LAST) as u:
                add_x(u - 2)
                unit(u)
            add_x(LAST - 2)
            add_x(LAST - 1)

        @block.scalar
        def _(act):
            def roots(m):
                act.wait_ge(var_ready, m + 1)
                act.activation(root[:, m], var[:, m], ACT.Sqrt).then_inc(root_ready, 1)
                act.wait_ge(demod_ready, m + 1)

            def evacuate_k(u, c):
                act.wait_ge(k_projected[c], u + 1)
                wait_positive(act, k_stored[c], 16 * (u - AHEAD + 1))
                for b in range(BPU):
                    q = BPU * u + b
                    last = act.activation(kT[:, u % AHEAD, c, b * SEQ:(b + 1) * SEQ], proj[c][:, b * SEQ:(b + 1) * SEQ], ACT.Identity,
                                          bias=out_bias[:, 0, c:c + 1], scale=demod[:, 0, c, q:q + 1])
                last.then_inc(k_evacuated[c], 1)

            def exponent(u, h):
                act.wait_ge(centered, 2 * u + h + 1)
                act.activation(attn[:, h], attn[:, h], ACT.Exp, scale=SCALE).then_inc(exp_ready, 1)

            def copy_turned(u, h):
                act.wait_ge(attn_turned, 2 * u + h + 1)
                wait_positive(act, mix_done, GROUPS * u + 2 * h - 2)
                n0 = h * OCTETS // 2
                for g in range(SIDES):
                    rows = slice(g * P // SIDES, (g + 1) * P // SIDES)
                    last = act.activation(a_stat[rows, n0:n0 + OCTETS // 2, g, :],
                                          turned[h][rows].rearrange("p t v h -> p (t v) h"), ACT.Copy)
                last.then_inc(a_stat_ready, 1)

            def copy_sj(u):
                act.wait_ge(k_sj_loaded, 16 * (u + 1))
                wait_positive(act, blocks2_act, 2 * (u - 1))
                wait_positive(act, blocks2_pool, 2 * u)
                act.activation(k_sjc[:], k_sj[:].rearrange("p d n -> p n d"), ACT.Copy).then_inc(k_sj_copied, 1)

            def store_k(u, c):
                act.wait_ge(k_evacuated[c], u + 1)
                wait_positive(act, k_stored[c], 16 * u)
                act.dma_start(k_scratch[u, :, c * P:(c + 1) * P, :].rearrange("s p n -> p s n"),
                              kT[:, u % AHEAD, c, :].rearrange("p (s n) -> p s n", s=PACK)).then_inc(k_stored[c], 16)

            def spread2(u, h):
                act.wait_ge(k_sj_copied, u + 1)
                wait_positive(act, mix_done, GROUPS * u + 2 * h - 2)
                n0 = h * OCTETS // 2
                for s in range(ACT_TERMS):
                    last = act.activation(blocks2[:, s, n0:n0 + OCTETS // 2, 0:DIM],
                                          k_sjc[:, n0:n0 + OCTETS // 2, :],
                                          ACT.Copy, scale=four_mask[:, s:s + 1])
                last.then_inc(blocks2_act, 1)

            def evacuate_y(u, c):
                act.wait_ge(y_projected[c], u + 1)
                wait_positive(act, y_stored[c], 16 * u)
                for b in range(BPU):
                    q = BPU * u + b
                    last = act.activation(of_batch(yT[:, c, :], b), of_batch(proj[c][:], b), ACT.Identity,
                                          bias=out_bias[:, 1, c:c + 1], scale=demod[:, 1, c, bass.ds(q, 1)])
                last.then_inc(y_evacuated[c], 1)

            def spread1_share(u, h):
                act.wait_ge(k_stat_ready, 2 * u + h + 1)
                wait_positive(act, scored, 2 * u + h - 1)
                n0 = h * OCTETS // 2
                for s in range(DVE_TERMS[h], PACK):
                    last = act.activation(blocks1[:, s, n0:n0 + OCTETS // 2, :], k_cols[:, n0:n0 + OCTETS // 2, :],
                                          ACT.Copy, scale=block_mask[:, s:s + 1])
                last.then_inc(blocks1_act, 1)

            roots(0)
            for c in range(CH):
                evacuate_k(0, c)
                store_k(0, c)
            roots(1)
            evacuate_k(1, 0)
            store_k(1, 0)
            evacuate_k(1, 1)
            act.activation(unread[:], block_mask[:, 0:1], ACT.Exp)
            for u in (2, 3):
                for c in range(CH):
                    evacuate_k(u, c)
            act.wait_ge(k_sd_loaded, PACK * 16)
            store_k(1, 1)
            act.wait_ge(blocks_zeroed, 1)
            spread1_share(0, 0)
            copy_sj(0)
            spread1_share(0, 1)
            for c in range(CH):
                evacuate_k(4, c)
            act.wait_ge(pads_zeroed, 2)
            act.wait_ge(ones_set, FOUR)

            def bias_last():
                act.wait_ge(x_loaded[LAST], 16)
                for h in range(2):
                    for c in range(CH):
                        act.activation(x_last[:, c, h * HALF_UNIT:(h + 1) * HALF_UNIT].rearrange("p (c s t) -> p c s t", c=FOUR, s=PACK),
                                       xT[:, LAST, c, :].rearrange("p (s a t c) -> p a c s t", s=PACK, a=2, c=FOUR)[:, h],
                                       ACT.Identity, bias=out_bias[:, 1, c:c + 1]).then_inc(x_biased, 1)

            def unit(u, ahead=False, spread=True):
                exponent(u, 0)
                if ahead and u == 0:
                    for c in range(CH):
                        store_k(2, c)
                exponent(u, 1)
                for c in range(CH):
                    copy_turned(u, c)
                    if ahead:
                        evacuate_k(u + AHEAD, c)
                    else:
                        evacuate_y(u - 2, c)
                if spread:
                    spread1_share(u + 1, 0)
                    spread1_share(u + 1, 1)
                if ahead:
                    for c in range(CH):
                        store_k(2 * u + 2 if u > 0 else 3, c)
                if spread:
                    copy_sj(u + 1)
                    spread2(u + 1, 0)
                    spread2(u + 1, 1)
                if ahead and u > 0:
                    for c in range(CH):
                        store_k(2 * u + 3, c)
                if ahead and 0 < u < PHASE - 1:
                    for c in range(CH):
                        evacuate_y(u - 1, c)
                    bias_last()

            for u in range(PHASE):
                unit(u, ahead=True)
            with act.Fori(PHASE, LAST) as u:
                unit(u)
            unit(LAST, spread=False)
            for c in range(CH):
                act.wait_ge(y_added[c], LAST - 1)
                act.dma_start(y[LAST - 2, c], yT[:, c, :]).then_inc(y_stored[c], 16)
            for c in range(CH):
                evacuate_y(LAST - 1, c)
            for c in range(CH):
                act.wait_ge(y_added[c], LAST)
                act.dma_start(y[LAST - 1, c], yT[:, c, :]).then_inc(y_stored[c], 16)


def kernel(x, cond_512, L0_cond_k_aff_w, L0_cond_k_aff_b, L0_cond_k_w, L0_cond_k_b,
           L0_cond_o_aff_w, L0_cond_o_aff_b, L0_cond_o_w, L0_cond_o_b):
    import numpy as np
    import concourse.bacc as bacc
    from concourse.bass_utils import run_bass_kernel_spmd

    fp32 = mybir.dt.float32
    x_in = np.ascontiguousarray(np.asarray(x).reshape(UNITS, UNIT, CH, P).transpose(0, 2, 3, 1))

    def column(v):
        return np.asarray(v).reshape(CH, P).T

    mask = np.repeat(np.eye(PACK, dtype=np.float32), DIM, axis=0)
    params = np.ascontiguousarray(np.concatenate([
        np.asarray(L0_cond_k_aff_w).T, np.asarray(cond_512).T,
        column(L0_cond_k_aff_b), column(L0_cond_o_aff_b), column(L0_cond_k_b), column(L0_cond_o_b),
        mask, np.tile(mask[0:P // SIDES, 0:FOUR], (SIDES, 1)), np.asarray(L0_cond_o_aff_w).T, np.eye(P, dtype=np.float32)], axis=1))
    weights = np.ascontiguousarray(np.stack([np.asarray(L0_cond_k_w).T, np.asarray(L0_cond_o_w).T]))

    nc = bacc.Bacc("TRN2", target_bir_lowering=False, num_devices=1)
    arrays = {"x_in": x_in, "params": params, "weights": weights}
    aps = [nc.dram_tensor(name, a.shape, fp32, kind="ExternalInput").ap() for name, a in arrays.items()]
    y = nc.dram_tensor("y", (LAST, CH, P, UNIT), fp32, kind="ExternalOutput").ap()
    y_last = nc.dram_tensor("y_last", (2, CH, P, HALF_UNIT), fp32, kind="ExternalOutput").ap()
    build(nc, *aps, y, y_last)
    result = run_bass_kernel_spmd(nc, [arrays], core_ids=[0])
    out = result.results[0]["y"].reshape(LAST, FEAT, FOUR, UNIT // FOUR).transpose(0, 3, 2, 1)
    last = result.results[0]["y_last"].reshape(2, FEAT, FOUR, PACK, HT * 2).transpose(3, 0, 4, 2, 1)
    return np.concatenate([out.reshape(-1, FEAT), last.reshape(-1, FEAT)]).reshape(BATCH, SEQ, FEAT)
```
